# Optimizing a Trainium2 kernel written in Bass

```python
import numpy as np
import jax
import jax.numpy as jnp

def _softmax(x, axis=-1):
    return jax.nn.softmax(x, axis=axis)

def _gelu(x):
    return jax.nn.gelu(x, approximate=True)

def _silu(x):
    return jax.nn.silu(x)

def _sigmoid(x):
    return jax.nn.sigmoid(x)

def _layernorm(x, axis=-1, eps=1e-05):
    m = jnp.mean(x, axis=axis, keepdims=True)
    v = jnp.var(x, axis=axis, keepdims=True)
    return (x - m) / jnp.sqrt(v + eps)

def _scatter_add(tgt, idx, src, axis=0):
    return tgt.at[idx].add(src)

def _segment_sum(src, seg, n):
    return jax.ops.segment_sum(src, seg, n)
kernel_name = 'mk_adaln_attn_ffn_d1_seqx_r8_38d985'

def setup_inputs(seed: int=0):
    np.random.seed(seed)
    _w = jnp.asarray

    def _rec_inputs():
        import jax
        import jax.numpy as jnp
        _rk = jax.random.key(seed)
        x = -7.109e-05 + 0.9999 * jax.random.normal(jax.random.fold_in(_rk, 1), (128, 32, 512), jnp.float32)
        _lenS = 32 - jax.random.randint(jax.random.fold_in(_rk, 7), (128,), 0, max(1, 32 // 4) + 1, jnp.int32)
        _lenS2 = 32 - jax.random.randint(jax.random.fold_in(_rk, 8), (128,), 0, max(1, 32 // 4) + 1, jnp.int32)
        itok_B_0_15 = jax.random.randint(jax.random.fold_in(_rk, 11), (128,), 0, 16, jnp.int32)
        itok_B_3_7 = jax.random.randint(jax.random.fold_in(_rk, 12), (128,), 3, 8, jnp.int32)
        return (x, itok_B_0_15, itok_B_3_7)
    x, itok_B_0_15, itok_B_3_7 = _rec_inputs()

    def _L0_cond_setup():
        import jax, jax.numpy as jnp
        import numpy as np
        B, C, T = (64, 32, 512)
        S, D = (16, 32)
        key = jax.random.key(seed)
        k1, k2, k3 = jax.random.split(key, 3)
        x = jax.random.normal(k1, (B, C, T), dtype=jnp.float32)
        condition = jax.random.randint(k2, (B,), 0, S, dtype=jnp.int64)
        bound = float(np.sqrt(6.0 / C))
        weights = jax.random.uniform(k3, (S, C, D), dtype=jnp.float32, minval=-bound, maxval=bound)
        return {'x': x, 'condition': condition, 'weights': weights}
    _L0_cond_all = _L0_cond_setup()
    _L0_cond_in = {k: v for k, v in _L0_cond_all.items() if k in ('weights',)}
    del _L0_cond_all

    def _L0_attn_setup():
        import jax, jax.numpy as jnp
        import numpy as np
        import math
        D_MODEL = 512
        N_HEADS = 32
        HEAD_DIM = D_MODEL // N_HEADS
        CLIP_QKV = 8.0
        ALIBI_BIAS_MAX = 8
        LN_EPS = 1e-05

        def _alibi_slopes(total_num_heads: int, alibi_bias_max: int) -> jnp.ndarray:
            next_p2 = 2 ** math.ceil(math.log2(total_num_heads))
            m = jnp.arange(1, next_p2 + 1, dtype=jnp.float32) * (alibi_bias_max / next_p2)
            slopes = 1.0 / jnp.power(2.0, m)
            if next_p2 != total_num_heads:
                slopes = jnp.concatenate([slopes[1::2], slopes[::2]])[:total_num_heads]
            return slopes

        def _layer_norm(x, w, b):
            mu = jnp.mean(x, axis=-1, keepdims=True)
            var = jnp.var(x, axis=-1, keepdims=True)
            return (x - mu) * jax.lax.rsqrt(var + LN_EPS) * w + b
        key = jax.random.key(seed)
        k0, k1, k2 = jax.random.split(key, 3)
        B, S = (2, 256)
        return {'hidden_states': jax.random.normal(k0, (B, S, D_MODEL), dtype=jnp.float32), 'w_qkv': jax.random.normal(k1, (3 * D_MODEL, D_MODEL), dtype=jnp.float32) * 0.02, 'q_ln_w': jnp.ones((D_MODEL,), jnp.float32), 'q_ln_b': jnp.zeros((D_MODEL,), jnp.float32), 'k_ln_w': jnp.ones((D_MODEL,), jnp.float32), 'k_ln_b': jnp.zeros((D_MODEL,), jnp.float32), 'w_out': jax.random.normal(k2, (D_MODEL, D_MODEL), dtype=jnp.float32) * 0.02}
    _L0_attn_all = _L0_attn_setup()
    _L0_attn_in = {k: v for k, v in _L0_attn_all.items() if k in ('w_qkv', 'q_ln_w', 'q_ln_b', 'k_ln_w', 'k_ln_b', 'w_out')}
    del _L0_attn_all

    def _L0_cond2_setup():
        import jax, jax.numpy as jnp
        import numpy as np
        MAX_LORAS, OUT, IN = (8, 512, 512)
        B, S = (4, 256)
        key = jax.random.key(seed)
        k1, k2, k3 = jax.random.split(key, 3)
        x = jax.random.normal(k1, (B, S, IN), dtype=jnp.float32)
        weight = jax.random.normal(k2, (MAX_LORAS, OUT, IN), dtype=jnp.float32) * 0.02
        adapter_ids = jax.random.randint(k3, (B,), 0, MAX_LORAS, dtype=jnp.int32)
        return {'x': x, 'weight': weight, 'adapter_ids': adapter_ids}
    _L0_cond2_all = _L0_cond2_setup()
    _L0_cond2_in = {k: v for k, v in _L0_cond2_all.items() if k in ('weight',)}
    del _L0_cond2_all

    def _L0_ffn_setup():
        import jax, jax.numpy as jnp
        import numpy as np
        HID, INT, LAT, NE, K = (512, 1024, 256, 8, 2)
        LN_EPS = 1e-05

        def _layernorm(x, gamma, beta):
            mu = jnp.mean(x, axis=-1, keepdims=True)
            var = jnp.var(x, axis=-1, keepdims=True)
            return (x - mu) * jax.lax.rsqrt(var + LN_EPS) * gamma + beta
        key = jax.random.key(seed)
        ks = jax.random.split(key, 8)
        s = lambda d: 1.0 / np.sqrt(d)
        return {'hidden_states': jax.random.normal(ks[0], (4, 256, HID), jnp.float32), 'gate_w': jax.random.normal(ks[1], (HID, NE), jnp.float32) * s(HID), 'up_w': jax.random.normal(ks[2], (HID, INT), jnp.float32) * s(HID), 'down_w': jax.random.normal(ks[3], (INT, HID), jnp.float32) * s(INT), 'fc1_w': jax.random.normal(ks[4], (HID, LAT), jnp.float32) * s(HID), 'fc2_w': jax.random.normal(ks[5], (LAT, HID), jnp.float32) * s(LAT), 'expert_w': jax.random.normal(ks[6], (LAT, LAT), jnp.float32), 'ln_gamma': jnp.ones((HID,), jnp.float32), 'ln_beta': jnp.zeros((HID,), jnp.float32)}
    _L0_ffn_all = _L0_ffn_setup()
    _L0_ffn_in = {k: v for k, v in _L0_ffn_all.items() if k in ('gate_w', 'up_w', 'down_w', 'fc1_w', 'fc2_w', 'expert_w', 'ln_gamma', 'ln_beta')}
    del _L0_ffn_all
    return {'x': x, 'itok_B_0_15': itok_B_0_15, 'itok_B_3_7': itok_B_3_7, 'L0_cond_weights': _L0_cond_in['weights'], 'L0_attn_w_qkv': _L0_attn_in['w_qkv'], 'L0_attn_q_ln_w': _L0_attn_in['q_ln_w'], 'L0_attn_q_ln_b': _L0_attn_in['q_ln_b'], 'L0_attn_k_ln_w': _L0_attn_in['k_ln_w'], 'L0_attn_k_ln_b': _L0_attn_in['k_ln_b'], 'L0_attn_w_out': _L0_attn_in['w_out'], 'L0_cond2_weight': _L0_cond2_in['weight'], 'L0_ffn_gate_w': _L0_ffn_in['gate_w'], 'L0_ffn_up_w': _L0_ffn_in['up_w'], 'L0_ffn_down_w': _L0_ffn_in['down_w'], 'L0_ffn_fc1_w': _L0_ffn_in['fc1_w'], 'L0_ffn_fc2_w': _L0_ffn_in['fc2_w'], 'L0_ffn_expert_w': _L0_ffn_in['expert_w'], 'L0_ffn_ln_gamma': _L0_ffn_in['ln_gamma'], 'L0_ffn_ln_beta': _L0_ffn_in['ln_beta']}

def reference(x, itok_B_0_15, itok_B_3_7, L0_cond_weights, L0_attn_w_qkv, L0_attn_q_ln_w, L0_attn_q_ln_b, L0_attn_k_ln_w, L0_attn_k_ln_b, L0_attn_w_out, L0_cond2_weight, L0_ffn_gate_w, L0_ffn_up_w, L0_ffn_down_w, L0_ffn_fc1_w, L0_ffn_fc2_w, L0_ffn_expert_w, L0_ffn_ln_gamma, L0_ffn_ln_beta):
    import jax
    import jax.numpy as jnp

    def _L0_cond_ref(x, condition, weights):
        import jax, jax.numpy as jnp
        import numpy as np
        B, C, T = (64, 32, 512)
        S, D = (16, 32)
        W = weights[condition]
        return jnp.einsum('bct,bcd->bdt', x, W)

    def _L0_attn_ref(hidden_states, w_qkv, q_ln_w, q_ln_b, k_ln_w, k_ln_b, w_out):
        import jax, jax.numpy as jnp
        import numpy as np
        import math
        D_MODEL = 512
        N_HEADS = 32
        HEAD_DIM = D_MODEL // N_HEADS
        CLIP_QKV = 8.0
        ALIBI_BIAS_MAX = 8
        LN_EPS = 1e-05

        def _alibi_slopes(total_num_heads: int, alibi_bias_max: int) -> jnp.ndarray:
            next_p2 = 2 ** math.ceil(math.log2(total_num_heads))
            m = jnp.arange(1, next_p2 + 1, dtype=jnp.float32) * (alibi_bias_max / next_p2)
            slopes = 1.0 / jnp.power(2.0, m)
            if next_p2 != total_num_heads:
                slopes = jnp.concatenate([slopes[1::2], slopes[::2]])[:total_num_heads]
            return slopes

        def _layer_norm(x, w, b):
            mu = jnp.mean(x, axis=-1, keepdims=True)
            var = jnp.var(x, axis=-1, keepdims=True)
            return (x - mu) * jax.lax.rsqrt(var + LN_EPS) * w + b
        B, S, D = hidden_states.shape
        qkv = jnp.einsum('bsd,ed->bse', hidden_states, w_qkv)
        qkv = jnp.clip(qkv, -CLIP_QKV, CLIP_QKV)
        q, k, v = jnp.split(qkv, 3, axis=-1)
        q = _layer_norm(q, q_ln_w, q_ln_b)
        k = _layer_norm(k, k_ln_w, k_ln_b)
        q = q.reshape(B, S, N_HEADS, HEAD_DIM)
        k = k.reshape(B, S, N_HEADS, HEAD_DIM)
        v = v.reshape(B, S, N_HEADS, HEAD_DIM)
        scale = HEAD_DIM ** (-0.5)
        scores = jnp.einsum('bqhd,bkhd->bhqk', q, k) * scale
        pos = jnp.arange(S)
        rel = pos[None, :] - pos[:, None]
        slopes = _alibi_slopes(N_HEADS, ALIBI_BIAS_MAX)
        bias = slopes[:, None, None] * rel.astype(jnp.float32)
        causal = rel <= 0
        scores = jnp.where(causal[None, None], scores + bias[None], -jnp.inf)
        probs = jax.nn.softmax(scores, axis=-1)
        attn = jnp.einsum('bhqk,bkhd->bqhd', probs, v).reshape(B, S, D)
        return jnp.einsum('bsd,ed->bse', attn, w_out)

    def _L0_cond2_ref(x, weight, adapter_ids):
        import jax, jax.numpy as jnp
        import numpy as np
        MAX_LORAS, OUT, IN = (8, 512, 512)
        B, S = (4, 256)
        w = weight[adapter_ids]
        return jnp.einsum('bsi,boi->bso', x, w)

    def _L0_ffn_ref(hidden_states, gate_w, up_w, down_w, fc1_w, fc2_w, expert_w, ln_gamma, ln_beta):
        import jax, jax.numpy as jnp
        import numpy as np
        HID, INT, LAT, NE, K = (512, 1024, 256, 8, 2)
        LN_EPS = 1e-05

        def _layernorm(x, gamma, beta):
            mu = jnp.mean(x, axis=-1, keepdims=True)
            var = jnp.var(x, axis=-1, keepdims=True)
            return (x - mu) * jax.lax.rsqrt(var + LN_EPS) * gamma + beta
        logits = jnp.einsum('bsh,he->bse', hidden_states, gate_w)
        routing_weights, selected_experts = jax.lax.top_k(logits, K)
        h = jax.nn.relu(jnp.einsum('bsh,hi->bsi', hidden_states, up_w)) ** 2
        shared_out = jnp.einsum('bsi,ih->bsh', h, down_w)
        x_latent = jnp.einsum('bsh,hl->bsl', hidden_states, fc1_w)
        expert_out = jnp.einsum('bsl,lm->bsm', x_latent, expert_w)
        moe_out = expert_out * jnp.sum(routing_weights, axis=-1, keepdims=True)
        routed_out = jnp.einsum('bsl,lh->bsh', moe_out, fc2_w)
        return _layernorm(shared_out + routed_out, ln_gamma, ln_beta)
    x = x + _L0_attn_ref(_L0_cond_ref(x, itok_B_0_15, L0_cond_weights), L0_attn_w_qkv, L0_attn_q_ln_w, L0_attn_q_ln_b, L0_attn_k_ln_w, L0_attn_k_ln_b, L0_attn_w_out)
    x = x + _L0_ffn_ref(_L0_cond2_ref(x, L0_cond2_weight, itok_B_3_7), L0_ffn_gate_w, L0_ffn_up_w, L0_ffn_down_w, L0_ffn_fc1_w, L0_ffn_fc2_w, L0_ffn_expert_w, L0_ffn_ln_gamma, L0_ffn_ln_beta)
    return x

_drawn_inputs = setup_inputs


def setup_inputs(seed=0):
    import zlib

    import numpy as np

    out = dict(_drawn_inputs(seed))
    spreads = {'L0_attn_q_ln_w': (1.0, 0.6),
     'L0_attn_q_ln_b': (0.0, 0.548),
     'L0_attn_k_ln_w': (1.0, 0.574),
     'L0_attn_k_ln_b': (0.0, 0.8),
     'L0_ffn_ln_gamma': (1.0, 0.2),
     'L0_ffn_ln_beta': (0.0, 0.1)}
    factors = {}
    for name, (base, spread) in spreads.items():
        noise = np.random.default_rng([zlib.crc32(name.encode()), seed]).standard_normal(out[name].shape)
        drawn = base * np.exp(spread * noise) if base else spread * noise
        out[name] = jnp.asarray(drawn.astype(out[name].dtype))
    for name, factor in factors.items():
        out[name] = (out[name] * factor).astype(out[name].dtype)
    return out
```

```python
from contextlib import ExitStack

import numpy as np

import concourse.bass as bass
from concourse import mybir

F32 = mybir.dt.float32
F32R = mybir.dt.float32r
BF16 = mybir.dt.bfloat16
I32 = mybir.dt.int32
ALU = mybir.AluOpType
ACT = mybir.ActivationFunctionType
AX = mybir.AxisListType

P = 128
BATCHES, SEQ, DM = 128, 32, 512
TOKENS = BATCHES * SEQ
BPT = P // SEQ
TILES = TOKENS // P
KC = DM // P
HEADS, HD = 32, 16
HPC = P // HD
HG = HEADS // BPT
STYLES = 16
ADAPTERS = 8
SLOTS = (BATCHES + ADAPTERS * (BPT - 1)) // BPT
INNER = 1024
FC = INNER // P
LAT = 256
LC = LAT // P
EXPERTS = 8
GROUP = 4
GROUPS = TILES // GROUP
CLIP = 8.0
SCALE = HD ** -0.5
EPS = 1e-5
MASKED = -1e30
ABSENT = 2.0 ** 17

C_BIAS = 0
C_IDENT = C_BIAS + HEADS * SEQ
C_KMASK = C_IDENT + P
C_VMASK = C_KMASK + HPC * SEQ
VW = BPT * HD + BPT
C_WMASK = C_VMASK + VW
C_ROW = C_WMASK + P
C_SLOT = C_ROW + P
C_VAL = C_SLOT + SLOTS * BPT
C_COL = C_VAL + SEQ
C_PMOD = C_COL + 1
C_POW = C_PMOD + 1
C_SIZE = C_POW + 2


def constants():
    p = np.arange(P)
    q = p % SEQ
    c = np.zeros((P, C_SIZE), np.float32)
    m = np.arange(1, HEADS + 1, dtype=np.float32) * np.float32(8 / HEADS)
    slopes = (np.float32(1.0) / np.power(np.float32(2.0), m)).astype(np.float32)
    rel = (np.arange(SEQ)[None, :] - q[:, None]).astype(np.float32)
    bias = slopes[None, :, None] * rel[:, None, :]
    c[:, C_BIAS:C_IDENT] = np.where(rel[:, None, :] <= 0, bias, np.float32(MASKED)).reshape(P, -1)
    c[:, C_IDENT:C_KMASK] = np.eye(P)
    c[:, C_KMASK:C_VMASK] = np.repeat(p[:, None] // HD == np.arange(HPC)[None, :], SEQ, axis=1)
    own = p[:, None] // SEQ == np.arange(BPT)[None, :]
    c[:, C_VMASK:C_VMASK + BPT * HD] = np.repeat(own, HD, axis=1)
    c[:, C_VMASK + BPT * HD:C_WMASK] = own
    c[:, C_WMASK:C_ROW] = np.repeat(own, SEQ, axis=1)
    c[:, C_ROW:C_SLOT] = p[None, :]
    c[:, C_SLOT:C_VAL] = np.arange(SLOTS * BPT)[None, :]
    c[:, C_VAL:C_COL] = (SEQ * p - ABSENT)[:, None]
    c[:, C_COL] = p
    c[:, C_PMOD] = q
    c[:, C_POW:C_POW + 2] = -0.5
    return c


def program(nc, x, style_ids, adapter_ids, style_w, wqkv, wo, qk_ln, w2, w_up, w_down, fc1t, expert,
            fc2, gate, ffn_ln, consts, out):
    x1_rows = nc.dram_tensor("x1_rows", [TOKENS, DM], F32, kind="Internal").ap()
    y_rows = nc.dram_tensor("y_rows", [TOKENS, DM], F32, kind="Internal").ap()
    top = ExitStack()

    def tiles_in(stack):
        def sb(name, shape, dt=F32):
            return stack.enter_context(nc.sbuf_tensor(name, shape, dt))
        return sb

    sb = tiles_in(top)

    def psum(name, shape, dt=F32):
        return top.enter_context(nc.psum_tensor(name, shape, dt))

    def sem(name):
        return top.enter_context(nc.semaphore(name))

    cst = sb("cst", [P, C_SIZE])
    ident = cst[:, C_IDENT:C_KMASK]
    bias = cst[:, C_BIAS:C_IDENT].rearrange("p (h k) -> p h k", h=HEADS)
    kmask = sb("kmask", [P, HPC * SEQ], BF16)
    vmask = sb("vmask", [P, VW], BF16)
    style_gathered = sb("style_gathered", [P, TILES, SEQ])
    qkln = sb("qkln", [P, 4 * KC])
    slot_rows = sb("slot_rows", [P, SLOTS], I32)
    slot_adapter = sb("slot_adapter", [1, SLOTS], I32)
    bank = [psum(f"bank{i}", [P, DM]) for i in range(2, 8)]
    pair = psum("pair", [P, 2, DM])
    B2, B3, B4, B5, B6, B7 = (b[:, :] for b in bank)

    weights = ExitStack()
    wsb = tiles_in(weights)
    wqkv_hi = wsb("wqkv_hi", [P, 3, KC, DM], F32R)
    wqkv_lo = wsb("wqkv_lo", [P, 3, KC, DM], F32R)
    wo_hi = wsb("wo_hi", [P, BPT, DM], F32R)
    wo_lo = wsb("wo_lo", [P, BPT, DM], F32R)

    prep = ExitStack()
    psb = tiles_in(prep)
    stage = [psb(f"stage{i}", [P, KC, DM]) for i in range(4)]
    ids_row = psb("ids_row", [P, BATCHES], I32)
    style_row = psb("style_row", [P, BATCHES], I32)
    ids_col = psb("ids_col", [P, 1], I32)
    idr = psb("idr", [P, BATCHES])
    idc = psb("idc", [P, 1])
    keyr = psb("keyr", [P, BATCHES])
    keyc = psb("keyc", [P, 1])
    before = psb("before", [P, BATCHES])
    after = psb("after", [P, BATCHES])
    same = psb("same", [P, BATCHES])
    within = psb("within", [P, 1])
    within_i = psb("within_i", [P, 1], I32)
    place_i = psb("place_i", [P, 1], I32)
    place = psb("place", [P, 1])
    first = psb("first", [P, 1])
    earlier = psb("earlier", [P, 1])
    slot_no = psb("slot_no", [P, 1])
    column = psb("column", [P, 1])
    onehot = psb("onehot", [P, SLOTS * BPT])
    slot_f = psb("slot_f", [P, SLOTS])
    adapter_f = psb("adapter_f", [1, SLOTS])
    stylef = psb("stylef", [P, TILES])
    style_idx = psb("style_idx", [P, TILES], I32)

    s_cst = sem("s_cst")
    s_ids = sem("s_ids")
    s_stage = [sem(f"s_stage{i}") for i in range(4)]
    s_whi = sem("s_whi")
    s_wlo = sem("s_wlo")
    s_t = sem("s_t")
    s_tp = sem("s_tp")
    s_gather = sem("s_gather")

    with nc.Block() as block:
        @block.sync
        def _(e):
            e.dma_start(cst[:, :], consts).then_inc(s_cst, 16)
            for dst, src in ((ids_row[:, :], adapter_ids.broadcast_to([P, BATCHES])),
                             (style_row[:, :], style_ids.broadcast_to([P, BATCHES])),
                             (ids_col[:, :], adapter_ids.rearrange("o b -> b o")),
                             (qkln[:, :], qk_ln)):
                e.dma_start(dst, src).then_inc(s_ids, 16)
            for n in range(4):
                e.dma_start(stage[n][:, :, :], wqkv[:, n] if n < 3 else wo).then_inc(s_stage[n], 16)
            e.wait_ge(s_gather, 16 * TILES)

        @block.scalar
        def _(e):
            for n in range(4):
                e.wait_ge(s_stage[n], 16)
                dst = wqkv_hi[:, n] if n < 3 else wo_hi[:, :, :]
                e.activation(dst, stage[n][:, :, :], ACT.Copy).then_inc(s_whi, 1)

        @block.vector
        def _(e):
            steps = [0]

            def step(i):
                i.then_inc(s_t, 1)
                steps[0] += 1
                e.wait_ge(s_t, steps[0])

            e.wait_ge(s_cst, 16)
            e.wait_ge(s_ids, 64)
            row, col = cst[:, C_ROW:C_SLOT], cst[:, C_COL:C_COL + 1]
            for j in range(BPT):
                src = style_row[SEQ * j:SEQ * j + SEQ, j::BPT]
                e.tensor_scalar(stylef[SEQ * j:SEQ * j + SEQ, :], src, float(SEQ), None, ALU.mult) \
                    .then_inc(s_t, 1)
                steps[0] += 1
            e.wait_ge(s_t, steps[0])
            step(e.tensor_scalar(style_idx[:, :], stylef[:, :], cst[:, C_PMOD:C_PMOD + 1], None, ALU.add))
            assert steps[0] == BPT + 1
            step(e.tensor_copy(kmask[:, :], cst[:, C_KMASK:C_VMASK]))
            step(e.tensor_copy(vmask[:, :], cst[:, C_VMASK:C_WMASK]))
            step(e.tensor_copy(idr[:, :], ids_row[:, :]))
            step(e.tensor_copy(idc[:, :], ids_col[:, :]))
            step(e.scalar_tensor_tensor(keyr[:, :], idr[:, :], float(BATCHES), row, ALU.mult, ALU.add))
            step(e.scalar_tensor_tensor(keyc[:, :], idc[:, :], float(BATCHES), col, ALU.mult, ALU.add))
            step(e.tensor_scalar(before[:, :], keyr[:, :], keyc[:, 0:1], None, ALU.is_lt))
            step(e.tensor_scalar(after[:, :], keyr[:, :], keyc[:, 0:1], None, ALU.is_gt))
            step(e.tensor_scalar(same[:, :], idr[:, :], idc[:, 0:1], None, ALU.is_equal))
            step(e.tensor_tensor(same[:, :], same[:, :], before[:, :], ALU.mult))
            step(e.tensor_reduce(within[:, :], same[:, :], AX.X, ALU.add))
            step(e.tensor_copy(within_i[:, :], within[:, :]))
            step(e.tensor_scalar(place_i[:, :], within_i[:, :], BPT - 1, None, ALU.bitwise_and))
            step(e.tensor_copy(place[:, :], place_i[:, :]))
            step(e.tensor_scalar(first[:, :], place[:, :], 0.0, None, ALU.is_equal))
            e.wait_ge(s_tp, 1)
            step(e.tensor_copy(earlier[:, :], B2[:, 0:1]))
            step(e.scalar_tensor_tensor(slot_no[:, :], earlier[:, :], -1.0, first[:, :], ALU.add, ALU.add))
            step(e.scalar_tensor_tensor(column[:, :], slot_no[:, :], float(BPT), place[:, :],
                                        ALU.mult, ALU.add))
            step(e.tensor_scalar(onehot[:, :], cst[:, C_SLOT:C_VAL], column[:, 0:1], None, ALU.is_equal))
            e.wait_ge(s_tp, 2)
            step(e.tensor_scalar(slot_f[:, :], B3[:, 0:SLOTS], ABSENT, cst[:, C_PMOD:C_PMOD + 1],
                                 ALU.add, ALU.add))
            step(e.tensor_copy(slot_rows[:, :], slot_f[:, :]))
            step(e.tensor_copy(adapter_f[:, :], B4[0:1, 0:SLOTS]))
            step(e.tensor_copy(slot_adapter[:, :], adapter_f[:, :]))
            for n in range(4):
                e.wait_ge(s_whi, n + 1)
                hi, dst = (wqkv_hi[:, n], wqkv_lo[:, n]) if n < 3 else (wo_hi[:, :, :], wo_lo[:, :, :])
                e.tensor_tensor(dst, stage[n][:, :, :], hi.bitcast(F32), ALU.subtract).then_inc(s_wlo, 1)

        @block.gpsimd
        def _(e):
            e.wait_ge(s_t, BPT + 1)
            for i in range(TILES):
                e.indirect_dma_start(
                    out=style_gathered[:, i, :], out_offset=None, in_=style_w,
                    in_offset=bass.IndirectOffsetOnAxis(ap=style_idx[:, i:i + 1], axis=0),
                ).then_inc(s_gather, 16)

        @block.tensor
        def _(e):
            e.wait_ge(s_t, BPT + 1 + 15)
            e.matmul(B2[:, 0:1], after[:, :], first[:, :], start=True, stop=True).then_inc(s_tp, 1)
            e.wait_ge(s_t, BPT + 1 + 19)
            for j in range(BPT):
                e.matmul(B3[SEQ * j:SEQ * j + SEQ, 0:SLOTS], cst[:, C_VAL:C_COL], onehot[:, j::BPT],
                         start=True, stop=True)
            e.matmul(B4[0:1, 0:SLOTS], idc[:, :], onehot[:, 0::BPT], start=True, stop=True) \
                .then_inc(s_tp, 1)
    prep.close()

    XR, VR = 8, 5
    att = ExitStack()
    asb = tiles_in(att)
    xt = [asb(f"xt{i}", [P, DM]) for i in range(XR)]
    style_bd = [asb(f"style_bd{i}", [P, BPT, SEQ]) for i in range(2)]
    h_hi = [asb(f"h_hi{i}", [P, KC, P], F32R) for i in range(2)]
    h_lo = [asb(f"h_lo{i}", [P, KC, P], F32R) for i in range(2)]
    qn = [asb(f"qn{i}", [P, DM]) for i in range(2)]
    kn = [asb(f"kn{i}", [P, DM]) for i in range(2)]
    stats = [asb(f"stats{i}", [P, 2, 6]) for i in range(2)]
    mean_var = [asb(f"mean_var{i}", [P, 2, 2]) for i in range(2)]
    var_eps = [asb(f"var_eps{i}", [P, 2]) for i in range(2)]
    rstd = [asb(f"rstd{i}", [P, 2]) for i in range(2)]
    shift = [asb(f"shift{i}", [P, 2]) for i in range(2)]
    qT = asb("qT", [P, KC, P])
    kT = asb("kT", [P, KC, P])
    q_hi = asb("q_hi", [P, KC, P], BF16)
    q_lo = asb("q_lo", [P, KC, P], BF16)
    k_hi = asb("k_hi", [P, KC * P], BF16)
    k_lo = asb("k_lo", [P, KC * P], BF16)
    kx_hi = asb("kx_hi", [P, KC * BPT, HPC, SEQ], BF16)
    kx_lo = asb("kx_lo", [P, KC * BPT, HPC, SEQ], BF16)
    vf = [asb(f"vf{i}", [P, DM]) for i in range(2)]
    v_hi = [asb(f"v_hi{i}", [P, HEADS, HD], BF16) for i in range(VR)]
    v_lo = [asb(f"v_lo{i}", [P, HEADS, HD], BF16) for i in range(VR)]
    vx_hi = asb("vx_hi", [P, HEADS, VW], BF16)
    vx_lo = asb("vx_lo", [P, HEADS, VW], BF16)
    probs = asb("probs", [P, HEADS, SEQ])
    row_max = asb("row_max", [P, HEADS])
    probsT = asb("probsT", [P, HEADS * SEQ])
    p_hi = asb("p_hi", [P, HEADS * SEQ], BF16)
    p_lo = asb("p_lo", [P, HEADS * SEQ], BF16)
    recip = asb("recip", [P, 2, 4, BPT])
    on = asb("on", [P, BPT, HG, HD])
    o_hi = asb("o_hi", [P, BPT, P], F32R)
    o_lo = asb("o_lo", [P, BPT, P], F32R)
    x1t = [asb(f"x1t{i}", [P, DM]) for i in range(2)]

    a_x = [sem(f"a_load{i}") for i in range(XR)]
    a_store = [sem(f"a_store{i}") for i in range(2)]
    names = ("style", "h", "hhi", "hlo", "pq", "pk", "pv", "cq", "ck", "bn", "aggr", "eps", "rstd", "shift",
             "qn", "kn", "tq", "tk", "qT", "kT", "qhi", "qlo", "khi", "klo", "kxhi", "kxlo", "cv", "vhi",
             "vlo", "vxhi", "vxlo", "vx1", "s", "sb", "max", "sub", "exp", "pT", "phi", "plo", "o", "rec",
             "on", "ot", "ohi", "olo", "r", "x1")
    A = {n: sem(f"a_{n}") for n in names}
    PER = {"bn": 2, "sb": 2, "on": 2}
    T = TILES

    def upto(e, name, i):
        if i >= 0:
            e.wait_ge(A[name], PER.get(name, 1) * (i + 1))

    with nc.Block() as block:
        @block.sync
        def _(e):
            for i in range(T + 5):
                if i < T:
                    upto(e, "x1", i - XR)
                    e.dma_start(xt[i % XR][:, :], x[P * i:P * i + P, :]).then_inc(a_x[i % XR], 16)
                t = i - 5
                if t >= 0:
                    upto(e, "x1", t)
                    e.dma_start(x1_rows[P * t:P * t + P, :], x1t[t % 2][:, :]).then_inc(a_store[t % 2], 16)
            for n in range(2):
                e.wait_ge(a_store[n], 16 * (T // 2))

        @block.tensor
        def _(e):
            def style(t):
                e.wait_ge(a_x[t % XR], 16 * (t // XR + 1))
                upto(e, "style", t)
                upto(e, "hlo", t - 1)
                for c in range(KC):
                    m = e.matmul(B7[:, P * c:P * c + P], xt[t % XR][:, P * c:P * c + P],
                                 style_bd[t % 2][:, :, :].rearrange("p j d -> p (j d)"), start=True, stop=True)
                m.then_inc(A["h"], 1)

            def project(t, n, into, name):
                upto(e, "hlo", t)
                hi, lo = h_hi[t % 2], h_lo[t % 2]
                for c in range(KC):
                    for k, (a, b) in enumerate(((hi, wqkv_hi), (hi, wqkv_lo), (lo, wqkv_hi))):
                        m = e.matmul(into, a[:, c, :], b[:, n, c, :], start=(c == 0 and k == 0),
                                     stop=(c == KC - 1 and k == 2))
                m.then_inc(A[name], 1)

            def values(t):
                upto(e, "phi", t)
                upto(e, "plo", t)
                upto(e, "vxlo", t)
                e.wait_ge(A["vx1"], 1)
                upto(e, "sb", min(t + 1, T - 1))
                for g in range(HG):
                    dst = pair[:, g // 4, VW * (g % 4):VW * (g % 4) + VW]
                    for k, (a, b, w) in enumerate(((p_hi, vx_hi, VW), (p_lo, vx_hi, VW),
                                                   (p_hi, vx_lo, BPT * HD))):
                        for j in range(BPT):
                            h = BPT * g + j
                            m = e.matmul(dst[SEQ * j:SEQ * j + SEQ, 0:w], a[:, SEQ * h:SEQ * h + SEQ],
                                         b[:, h, 0:w], start=(k == 0), stop=(k == 2),
                                         skip_group_check=True)
                m.then_inc(A["o"], 1)

            def turn_values(t):
                upto(e, "on", t)
                upto(e, "olo", t - 1)
                for b in range(BPT):
                    m = e.transpose(B4[:, P * b:P * b + P],
                                    on[:, b, :, :].rearrange("p g d -> p (g d)"), ident)
                m.then_inc(A["ot"], 1)

            def out_project(t):
                upto(e, "olo", t)
                upto(e, "x1", t - 1)
                for j in range(BPT):
                    for k, (a, b) in enumerate(((o_hi, wo_hi), (o_hi, wo_lo), (o_lo, wo_hi))):
                        m = e.matmul(B6, a[:, j, :], b[:, j, :], start=(j == 0 and k == 0),
                                     stop=(j == BPT - 1 and k == 2))
                m.then_inc(A["r"], 1)

            def turn(t, src, done, into, name):
                upto(e, done, t)
                for c in range(KC):
                    m = e.transpose(into[:, P * c:P * c + P], src[:, P * c:P * c + P], ident)
                m.then_inc(A[name], 1)

            def scores(t):
                for n in ("qhi", "qlo", "kxhi", "kxlo"):
                    upto(e, n, t)
                upto(e, "on", t - 2)
                for c in range(KC):
                    dst = pair[:, c // 2, 256 * (c % 2):256 * (c % 2) + 256]
                    for k, (a, b) in enumerate(((q_hi, kx_hi), (q_lo, kx_hi), (q_hi, kx_lo))):
                        for j in range(BPT):
                            m = e.matmul(dst[SEQ * j:SEQ * j + SEQ, :], a[:, c, SEQ * j:SEQ * j + SEQ],
                                         b[:, BPT * c + j, :, :].rearrange("p h k -> p (h k)"),
                                         start=(k == 0), stop=(k == 2), skip_group_check=True)
                m.then_inc(A["s"], 1)

            style(0)
            for i in range(T + 4):
                live = lambda t: 0 <= t < T
                if i + 1 < T:
                    style(i + 1)
                if live(i):
                    upto(e, "cq", i - 1)
                    project(i, 0, B2, "pq")
                if live(i - 4):
                    values(i - 4)
                if live(i):
                    upto(e, "ck", i - 1)
                    upto(e, "qT", i - 2)
                    project(i, 1, B3, "pk")
                if live(i - 4):
                    turn_values(i - 4)
                if live(i):
                    upto(e, "cv", i - 1)
                    upto(e, "kT", i - 2)
                    project(i, 2, B5, "pv")
                if live(i - 4):
                    out_project(i - 4)
                if live(i - 1):
                    upto(e, "ck", min(i, T - 1))
                    turn(i - 1, qn[(i - 1) % 2], "qn", B3, "tq")
                    upto(e, "cv", min(i, T - 1))
                    turn(i - 1, kn[(i - 1) % 2], "kn", B5, "tk")
                if live(i - 2):
                    scores(i - 2)

        @block.scalar
        def _(e):
            for i in range(-1, T + 4):
                live = lambda t: 0 <= t < T
                t = i - 2
                if live(t):
                    upto(e, "tq", t)
                    upto(e, "qlo", t - 1)
                    for c in range(KC):
                        m = e.activation(qT[:, c, :], B3[:, P * c:P * c + P], ACT.Identity,
                                         bias=qkln[:, KC + c:KC + c + 1], scale=qkln[:, c:c + 1])
                    m.then_inc(A["qT"], 1)
                if live(i + 1):
                    t = i + 1
                    upto(e, "h", t)
                    upto(e, "pv", t - 2)
                    e.activation(h_hi[t % 2][:, :, :], B7.rearrange("p (c t) -> p c t", c=KC), ACT.Copy) \
                        .then_inc(A["hhi"], 1)
                t = i - 2
                if live(t):
                    upto(e, "tk", t)
                    upto(e, "klo", t - 1)
                    for c in range(KC):
                        m = e.activation(kT[:, c, :], B5[:, P * c:P * c + P], ACT.Identity,
                                         bias=qkln[:, 3 * KC + c:3 * KC + c + 1],
                                         scale=qkln[:, 2 * KC + c:2 * KC + c + 1])
                    m.then_inc(A["kT"], 1)
                    upto(e, "kT", t)
                    upto(e, "kxlo", t - 1)
                    e.activation(k_hi[:, :], kT[:, :, :].rearrange("p c t -> p (c t)"), ACT.Copy) \
                        .then_inc(A["khi"], 1)
                    upto(e, "qT", t)
                    upto(e, "s", t - 1)
                    e.activation(q_hi[:, :, :], qT[:, :, :], ACT.Copy).then_inc(A["qhi"], 1)
                t = i - 3
                if live(t):
                    upto(e, "sub", t)
                    e.activation(probs[:, :, :], probs[:, :, :], ACT.Exp).then_inc(A["exp"], 1)
                    upto(e, "pT", t)
                    upto(e, "o", t - 1)
                    e.activation(p_hi[:, :], probsT[:, :], ACT.Copy).then_inc(A["phi"], 1)
                t = i - 4
                if live(t):
                    upto(e, "ot", t)
                    upto(e, "r", t - 1)
                    e.activation(o_hi[:, :, :].rearrange("p j (b q) -> p j b q", b=BPT),
                                 B4.rearrange("p (b j q) -> p j b q", b=BPT, j=BPT), ACT.Copy) \
                        .then_inc(A["ohi"], 1)
                if live(i):
                    t = i
                    upto(e, "shift", t)
                    for n, buf in enumerate((qn, kn)):
                        b = buf[t % 2]
                        e.activation(b[:, :], b[:, :], ACT.Identity, bias=shift[t % 2][:, n:n + 1],
                                     scale=rstd[t % 2][:, n:n + 1]).then_inc(A[("qn", "kn")[n]], 1)
                    upto(e, "cv", t)
                    upto(e, "vxhi", t - VR)
                    e.activation(v_hi[t % VR][:, :, :], vf[t % 2][:, :].rearrange("p (h d) -> p h d", h=HEADS),
                                 ACT.Copy).then_inc(A["vhi"], 1)

        @block.vector
        def _(e):
            def clip(t, src, dst, name):
                e.tensor_scalar(dst, src, CLIP, -CLIP, ALU.min, ALU.max).then_inc(A[name], 1)

            e.tensor_copy(vx_hi[:, :, BPT * HD:VW], vmask[:, BPT * HD:VW].rearrange("p (o b) -> p o b", o=1)
                          .broadcast_to([P, HEADS, BPT])).then_inc(A["vx1"], 1)
            for i in range(-1, T + 4):
                live = lambda t: 0 <= t < T
                t = i - 3
                if live(t):
                    upto(e, "s", t)
                    upto(e, "pT", t - 1)
                    for n in range(2):
                        h = slice(16 * n, 16 * n + 16)
                        e.scalar_tensor_tensor(probs[:, h, :], pair[:, n, :].rearrange("p (h k) -> p h k", k=SEQ),
                                               SCALE, bias[:, h, :], ALU.mult, ALU.add).then_inc(A["sb"], 1)
                if live(i + 1):
                    t = i + 1
                    upto(e, "hhi", t)
                    upto(e, "pv", t - 2)
                    e.tensor_tensor(h_lo[t % 2][:, :, :], B7.rearrange("p (c t) -> p c t", c=KC),
                                    h_hi[t % 2][:, :, :].bitcast(F32), ALU.subtract).then_inc(A["hlo"], 1)
                t = i - 3
                if live(t):
                    upto(e, "sb", t)
                    upto(e, "sub", t - 1)
                    e.tensor_reduce(row_max[:, :], probs[:, :, :], AX.X, ALU.max).then_inc(A["max"], 1)
                if live(i):
                    t = i
                    upto(e, "pq", t)
                    upto(e, "tq", t - 2)
                    clip(t, B2, qn[t % 2][:, :], "cq")
                    upto(e, "cq", t)
                    e.bn_stats(stats[t % 2][:, 0, :], qn[t % 2][:, :]).then_inc(A["bn"], 1)
                t = i - 2
                if live(t):
                    upto(e, "khi", t)
                    upto(e, "s", t - 1)
                    wide = lambda a: a[:, :].rearrange("p (n o k) -> p n o k", o=1, k=SEQ) \
                        .broadcast_to([P, KC * BPT, HPC, SEQ])
                    mask = kmask[:, :].rearrange("p (o h k) -> p o h k", o=1, h=HPC) \
                        .broadcast_to([P, KC * BPT, HPC, SEQ])
                    e.tensor_tensor(kx_hi[:, :, :, :], wide(k_hi), mask, ALU.mult).then_inc(A["kxhi"], 1)
                    e.tensor_tensor(k_lo[:, :], kT[:, :, :].rearrange("p c t -> p (c t)"), k_hi[:, :],
                                    ALU.subtract).then_inc(A["klo"], 1)
                t = i - 4
                if live(t):
                    upto(e, "o", t)
                    o4 = pair[:, :, 0:4 * VW].rearrange("p n (g v) -> p n g v", g=4)
                    e.reciprocal(recip[:, :, :, :], o4[:, :, :, BPT * HD:VW]).then_inc(A["rec"], 1)
                    upto(e, "rec", t)
                    upto(e, "ot", t - 1)
                    for n in range(2):
                        e.tensor_tensor(on[:, :, 4 * n:4 * n + 4, :].rearrange("p b g d -> p g b d"),
                                        o4[:, n, :, 0:BPT * HD].rearrange("p g (b d) -> p g b d", b=BPT),
                                        recip[:, n, :, :].rearrange("p g (b o) -> p g b o", o=1)
                                        .broadcast_to([P, 4, BPT, HD]), ALU.mult).then_inc(A["on"], 1)
                t = i - 3
                if live(t):
                    upto(e, "exp", t)
                    upto(e, "plo", t - 1)
                    e.transpose(probsT[:, :], probs[:, :, :].rearrange("p h k -> p (h k)")) \
                        .then_inc(A["pT"], 1)
                if live(i):
                    t = i
                    upto(e, "pk", t)
                    upto(e, "tk", t - 2)
                    clip(t, B3, kn[t % 2][:, :], "ck")
                    upto(e, "ck", t)
                    e.bn_stats(stats[t % 2][:, 1, :], kn[t % 2][:, :]).then_inc(A["bn"], 1)
                    upto(e, "bn", t)
                    for n in range(2):
                        m = e.bn_aggr(mean_var[t % 2][:, n, :], stats[t % 2][:, n, :])
                    m.then_inc(A["aggr"], 1)
                    upto(e, "aggr", t)
                    e.tensor_scalar(var_eps[t % 2][:, :], mean_var[t % 2][:, :, 1], EPS, None, ALU.add) \
                        .then_inc(A["eps"], 1)
                t = i - 2
                if live(t):
                    upto(e, "klo", t)
                    e.tensor_tensor(kx_lo[:, :, :, :], wide(k_lo), mask, ALU.mult).then_inc(A["kxlo"], 1)
                    upto(e, "qhi", t)
                    e.tensor_tensor(q_lo[:, :, :], qT[:, :, :], q_hi[:, :, :], ALU.subtract) \
                        .then_inc(A["qlo"], 1)
                t = i - 4
                if live(t):
                    upto(e, "ohi", t)
                    upto(e, "r", t - 1)
                    e.tensor_tensor(o_lo[:, :, :].rearrange("p j (b q) -> p j b q", b=BPT),
                                    B4.rearrange("p (b j q) -> p j b q", b=BPT, j=BPT),
                                    o_hi[:, :, :].bitcast(F32).rearrange("p j (b q) -> p j b q", b=BPT),
                                    ALU.subtract).then_inc(A["olo"], 1)
                if live(i):
                    t = i
                    upto(e, "rstd", t)
                    upto(e, "kn", t - 2)
                    e.scalar_tensor_tensor(shift[t % 2][:, :], mean_var[t % 2][:, :, 0], -1.0,
                                           rstd[t % 2][:, :], ALU.mult, ALU.mult).then_inc(A["shift"], 1)
                    upto(e, "pv", t)
                    upto(e, "vlo", t - 2)
                    clip(t, B5, vf[t % 2][:, :], "cv")
                t = i - 3
                if live(t):
                    upto(e, "vlo", t)
                    upto(e, "vhi", t)
                    upto(e, "o", t - 1)
                    dims = [P, HEADS, BPT, HD]
                    own = vmask[:, 0:BPT * HD].rearrange("p (o b d) -> p o b d", o=1, b=BPT).broadcast_to(dims)
                    for vx, v, name in ((vx_hi, v_hi[t % VR], "vxhi"), (vx_lo, v_lo[t % VR], "vxlo")):
                        e.tensor_tensor(vx[:, :, 0:BPT * HD].rearrange("p h (b d) -> p h b d", b=BPT),
                                        v[:, :, :].rearrange("p h (o d) -> p h o d", o=1).broadcast_to(dims),
                                        own, ALU.mult).then_inc(A[name], 1)
                t = i - 4
                if live(t):
                    upto(e, "r", t)
                    if t >= 2:
                        e.wait_ge(a_store[t % 2], 16 * (t // 2))
                    e.tensor_tensor(x1t[t % 2][:, :], B6, xt[t % XR][:, :], ALU.add).then_inc(A["x1"], 1)

        @block.gpsimd
        def _(e):
            def style(t):
                upto(e, "h", t - 2)
                e.tensor_tensor(style_bd[t % 2][:, :, :],
                                style_gathered[:, t, :].rearrange("p (o d) -> p o d", o=1)
                                .broadcast_to([P, BPT, SEQ]),
                                cst[:, C_WMASK:C_ROW].rearrange("p (j d) -> p j d", j=BPT), ALU.mult) \
                    .then_inc(A["style"], 1)

            style(0)
            style(1)
            for i in range(T + 4):
                live = lambda t: 0 <= t < T
                t = i - 3
                if live(t):
                    upto(e, "max", t)
                    e.tensor_tensor(probs[:, :, :], probs[:, :, :],
                                    row_max[:, :].rearrange("p (h o) -> p h o", o=1)
                                    .broadcast_to([P, HEADS, SEQ]), ALU.subtract).then_inc(A["sub"], 1)
                if live(i + 2):
                    style(i + 2)
                if live(t):
                    upto(e, "phi", t)
                    upto(e, "o", t - 1)
                    e.tensor_tensor(p_lo[:, :], probsT[:, :], p_hi[:, :], ALU.subtract).then_inc(A["plo"], 1)
                if live(i):
                    t = i
                    upto(e, "eps", t)
                    e.tensor_tensor(rstd[t % 2][:, :], var_eps[t % 2][:, :], cst[:, C_POW:C_POW + 2], ALU.pow) \
                        .then_inc(A["rstd"], 1)
                    upto(e, "vhi", t)
                    upto(e, "vxlo", t - VR)
                    e.tensor_tensor(v_lo[t % VR][:, :, :], vf[t % 2][:, :].rearrange("p (h d) -> p h d", h=HEADS),
                                    v_hi[t % VR][:, :, :], ALU.subtract).then_inc(A["vlo"], 1)
    att.close()
    weights.close()

    up_hi = sb("up_hi", [P, KC, INNER], F32R)
    up_lo = sb("up_lo", [P, KC, INNER], F32R)
    down_hi = sb("down_hi", [P, FC, DM], F32R)
    down_lo = sb("down_lo", [P, FC, DM], F32R)
    route_hi = sb("route_hi", [P, KC, DM], F32R)
    route_lo = sb("route_lo", [P, KC, DM], F32R)
    gate_hl = sb("gate_hl", [P, KC, 2, EXPERTS], F32R)
    ad = ExitStack()
    dsb = tiles_in(ad)
    XG = 3
    w2t = dsb("w2t", [P, ADAPTERS * KC * DM])
    raw = [dsb(f"raw{i}", [P, KC, DM]) for i in range(2)]
    gate_raw = dsb("gate_raw", [P, KC, EXPERTS])
    fc1_sb = dsb("fc1_sb", [P, LC, DM])
    ex_sb = dsb("ex_sb", [P, LC, LAT])
    fc2_sb = dsb("fc2_sb", [P, LC, DM])
    latT = dsb("latT", [P, LC, DM])
    xg = [dsb(f"xg{i}", [P, DM]) for i in range(XG)]
    xgT = [dsb(f"xgT{i}", [P, DM]) for i in range(2)]
    ys = [dsb(f"ys{i}", [P, DM]) for i in range(2)]

    d_w2, d_raw, d_fc = sem("d_w2"), [sem("d_raw0"), sem("d_raw1")], sem("d_fc")
    d_zero, d_x, d_y = sem("d_zero"), [sem(f"d_x{i}") for i in range(XG)], [sem(f"d_y{i}") for i in range(2)]
    d_t, d_tc, d_m, d_mc = sem("d_t"), sem("d_tc"), sem("d_m"), sem("d_mc")
    d_hi, d_lo, d_lat, d_latc, d_route = sem("d_hi"), sem("d_lo"), sem("d_lat"), sem("d_latc"), sem("d_route")
    pieces = [(w_up[:, :, DM * n:DM * n + DM], up_hi[:, :, DM * n:DM * n + DM],
               up_lo[:, :, DM * n:DM * n + DM]) for n in range(INNER // DM)]
    pieces += [(w_down[:, KC * n:KC * n + KC, :], down_hi[:, KC * n:KC * n + KC, :],
                down_lo[:, KC * n:KC * n + KC, :]) for n in range(FC // KC)]
    PC = len(pieces)

    with nc.Block() as block:
        @block.sync
        def _(e):
            for a in range(ADAPTERS):
                e.dma_start(w2t[:, a * KC * DM:(a + 1) * KC * DM], w2[:, a].rearrange("p c o -> p (c o)")) \
                    .then_inc(d_w2, 16)
            for dst, src in ((fc1_sb, fc1t), (ex_sb, expert), (fc2_sb, fc2), (gate_raw, gate)):
                e.dma_start(dst[:, :, :], src).then_inc(d_fc, 16)
            for n, (src, _, _) in enumerate(pieces):
                if n >= 2:
                    e.wait_ge(d_lo, n - 1)
                e.dma_start(raw[n % 2][:, :, :], src).then_inc(d_raw[n % 2], 16)

        @block.gpsimd
        def _(e):
            def gather(s):
                if s >= XG:
                    e.wait_ge(d_t, s - XG + 1)
                e.indirect_dma_start(
                    out=xg[s % XG][:, :], out_offset=None, in_=x1_rows,
                    in_offset=bass.IndirectOffsetOnAxis(ap=slot_rows[:, s:s + 1], axis=0),
                    bounds_check=TOKENS - 1, oob_is_err=False).then_inc(d_x[s % XG], 16)

            for n in range(XG):
                e.memset(xg[n][:, :], 0.0).then_inc(d_zero, 1)
            e.wait_ge(d_zero, XG)
            for s in range(XG):
                gather(s)
            for s in range(SLOTS):
                e.wait_ge(d_mc, s + 1)
                e.indirect_dma_start(
                    out=y_rows, out_offset=bass.IndirectOffsetOnAxis(ap=slot_rows[:, s:s + 1], axis=0),
                    in_=ys[s % 2][:, :], in_offset=None,
                    bounds_check=TOKENS - 1, oob_is_err=False).then_inc(d_y[s % 2], 16)
                if s + XG < SLOTS:
                    gather(s + XG)
            for n in range(2):
                e.wait_ge(d_y[n], 16 * (SLOTS // 2))

        @block.tensor
        def _(e):
            def turn(s):
                e.wait_ge(d_x[s % XG], 16 * (s // XG + 1))
                if s >= 2:
                    e.wait_ge(d_tc, s - 1)
                for c in range(KC):
                    m = e.transpose((B4, B5)[s % 2][:, P * c:P * c + P], xg[s % XG][:, P * c:P * c + P], ident)
                m.then_inc(d_t, 1)

            turn(0)
            e.wait_ge(d_w2, 16 * ADAPTERS)
            for s in range(SLOTS):
                if s + 1 < SLOTS:
                    turn(s + 1)
                adapter = e.value_load(slot_adapter[0:1, s:s + 1], min_val=0, max_val=ADAPTERS - 1)
                e.wait_ge(d_tc, s + 1)
                if s >= 2:
                    e.wait_ge(d_mc, s - 1)
                for c in range(KC):
                    m = e.matmul((B2, B3)[s % 2], xgT[s % 2][:, P * c:P * c + P],
                                 w2t[:, bass.ds(adapter * (KC * DM) + c * DM, DM)],
                                 start=(c == 0), stop=(c == KC - 1))
                m.then_inc(d_m, 1)
                if s == 6:
                    e.wait_ge(d_fc, 64)
                    for m_ in range(LC):
                        for k in range(LC):
                            m = e.matmul((B6, B7)[m_], ex_sb[:, k, P * m_:P * m_ + P], fc1_sb[:, k, :],
                                         start=(k == 0), stop=(k == LC - 1))
                        m.then_inc(d_lat, 1)
                if 8 <= s < 8 + KC:
                    c = s - 8
                    e.wait_ge(d_latc, LC)
                    if c >= 2:
                        e.wait_ge(d_lo, PC + c - 1)
                    for k in range(LC):
                        m = e.matmul((B6, B7)[c % 2], latT[:, k, P * c:P * c + P], fc2_sb[:, k, :],
                                     start=(k == 0), stop=(k == LC - 1))
                    m.then_inc(d_route, 1)

        @block.scalar
        def _(e):
            def high(n):
                if n < PC:
                    e.wait_ge(d_raw[n % 2], 16 * (n // 2 + 1))
                    e.activation(pieces[n][1], raw[n % 2][:, :, :], ACT.Copy).then_inc(d_hi, 1)
                elif n < PC + KC:
                    e.wait_ge(d_route, n - PC + 1)
                    e.activation(route_hi[:, n - PC, :], (B6, B7)[(n - PC) % 2], ACT.Copy).then_inc(d_hi, 1)
                elif n == PC + KC:
                    e.wait_ge(d_fc, 64)
                    e.activation(gate_hl[:, :, 0, :], gate_raw[:, :, :], ACT.Copy).then_inc(d_hi, 1)

            todo = list(range(PC + KC + 1))
            for s in range(SLOTS):
                e.wait_ge(d_t, s + 1)
                if s >= 2:
                    e.wait_ge(d_m, s - 1)
                e.activation(xgT[s % 2][:, :], (B4, B5)[s % 2], ACT.Copy).then_inc(d_tc, 1)
                if s == 7:
                    e.wait_ge(d_lat, LC)
                    for m_ in range(LC):
                        m = e.activation(latT[:, m_, :], (B6, B7)[m_], ACT.Copy)
                        m.then_inc(d_latc, 1)
                if (s < 8 and s % 2 == 0) or 8 <= s < 13 or s == 14:
                    if todo:
                        high(todo.pop(0))
            assert not todo

        @block.vector
        def _(e):
            def low(n):
                e.wait_ge(d_hi, n + 1)
                if n < PC:
                    dst, src, hi = pieces[n][2], raw[n % 2][:, :, :], pieces[n][1]
                elif n < PC + KC:
                    dst, src, hi = route_lo[:, n - PC, :], (B6, B7)[(n - PC) % 2], route_hi[:, n - PC, :]
                else:
                    dst, src, hi = gate_hl[:, :, 1, :], gate_raw[:, :, :], gate_hl[:, :, 0, :]
                e.tensor_tensor(dst, src, hi.bitcast(F32), ALU.subtract).then_inc(d_lo, 1)

            todo = list(range(PC + KC + 1))
            for s in range(SLOTS):
                e.wait_ge(d_m, s + 1)
                if s >= 2:
                    e.wait_ge(d_y[s % 2], 16 * (s // 2))
                e.tensor_copy(ys[s % 2][:, :], (B2, B3)[s % 2]).then_inc(d_mc, 1)
                if ((s < 8 and s % 2 == 0) or 8 <= s < 13 or s == 14) and todo:
                    low(todo.pop(0))
            assert not todo
    ad.close()

    TOK = GROUP * P
    yt = [sb(f"yt{i}", [P, GROUP, DM]) for i in range(2)]
    x1g = [sb(f"x1g{i}", [P, DM]) for i in range(GROUP)]
    yT_hi = [sb(f"yT_hi{i}", [P, KC, TOK], F32R) for i in range(2)]
    yT_lo = [sb(f"yT_lo{i}", [P, KC, TOK], F32R) for i in range(2)]
    gates = sb("gates", [2 * EXPERTS, TOK])
    gates_t = sb("gates_t", [P, GROUP, 2 * EXPERTS])
    logits = sb("logits", [P, GROUP, EXPERTS])
    best = sb("best", [P, GROUP, 8])
    weight = [sb(f"weight{i}", [P, GROUP]) for i in range(2)]
    act = [sb(f"act{i}", [P, TOK]) for i in range(3)]
    u_hi = sb("u_hi", [P, FC, TOK], F32R)
    u_lo = sb("u_lo", [P, FC, TOK], F32R)
    lnw = sb("lnw", [P, 2, DM])
    total = [sb(f"total{i}", [P, DM]) for i in range(2)]
    fstats = sb("fstats", [P, 6])
    fmv = [sb(f"fmv{i}", [P, 2]) for i in range(2)]
    fve = [sb(f"fve{i}", [P, 1]) for i in range(2)]
    frstd = [sb(f"frstd{i}", [P, 1]) for i in range(2)]
    fshift = [sb(f"fshift{i}", [P, 1]) for i in range(2)]
    ot = [sb(f"ot{i}", [P, DM]) for i in range(3)]

    f_ln = sem("f_ln")
    f_y, f_x1 = [sem(f"f_y{i}") for i in range(2)], [sem(f"f_res{i}") for i in range(GROUP)]
    f_out = [sem(f"f_out{i}") for i in range(3)]
    fn = ("t", "hi", "lo", "g", "gc", "gt", "gtc", "log", "best", "w", "u", "relu", "act", "uhi", "ulo", "dr", "route", "tot",
          "bn", "aggr", "eps", "rstd", "shift", "norm", "gam", "bet", "res")
    S = {n: sem(f"f_{n}_") for n in fn}

    with nc.Block() as block:
        @block.sync
        def _(e):
            e.dma_start(lnw[:, :, :].rearrange("p a n -> p (a n)"), ffn_ln.broadcast_to([P, 2 * DM])) \
                .then_inc(f_ln, 16)

            def load(m):
                rows = slice(TOK * m, TOK * m + TOK)
                if m >= 2:
                    e.wait_ge(S["t"], KC * (m - 1))
                e.dma_start(yt[m % 2][:, :, :], y_rows[rows, :].rearrange("(t p) n -> p t n", p=P)) \
                    .then_inc(f_y[m % 2], 16)

            def load_x1(n):
                if n >= GROUP:
                    e.wait_ge(S["res"], n - GROUP + 1)
                e.dma_start(x1g[n % GROUP][:, :], x1_rows[P * n:P * n + P, :]).then_inc(f_x1[n % GROUP], 16)

            def store(t):
                e.wait_ge(S["res"], t + 1)
                e.dma_start(out[P * t:P * t + P, :], ot[t % 3][:, :]).then_inc(f_out[t % 3], 16)

            load(0)
            load(1)
            for n in range(GROUP):
                load_x1(n)
            for m in range(GROUPS):
                for t in range(GROUP):
                    n = GROUP * m + t
                    store(n)
                    if n + GROUP < TILES:
                        load_x1(n + GROUP)
                if m + 2 < GROUPS:
                    load(m + 2)
            for n in range(3):
                e.wait_ge(f_out[n], 16 * ((TILES - n + 2) // 3))

        @block.tensor
        def _(e):
            def turn(m):
                e.wait_ge(f_y[m % 2], 16 * (m // 2 + 1))
                for c in range(KC):
                    n = KC * m + c
                    if n >= 2:
                        e.wait_ge(S["lo"], n - 1)
                    if c < 2 and m:
                        e.wait_ge(S["gtc"], m)
                        e.wait_ge(S["gc"], m)
                    for t in range(GROUP):
                        k = e.transpose((B4, B5)[c % 2][:, P * t:P * t + P],
                                        yt[m % 2][:, t, P * c:P * c + P], ident)
                    k.then_inc(S["t"], 1)

            def gate_products(m):
                e.wait_ge(S["lo"], KC * (m + 1))
                for c in range(KC):
                    w = gate_hl[:, c, :, :].rearrange("p a n -> p (a n)")
                    for n, y in enumerate((yT_hi, yT_lo)):
                        k = e.matmul(B4[0:2 * EXPERTS, :], w, y[m % 2][:, c, :],
                                     start=(c == 0 and n == 0), stop=(c == KC - 1 and n == 1))
                k.then_inc(S["g"], 1)

            def turn_gates(m):
                e.wait_ge(S["gc"], m + 1)
                for t in range(GROUP):
                    k = e.transpose(B5[:, 2 * EXPERTS * t:2 * EXPERTS * (t + 1)],
                                    gates[:, P * t:P * t + P], cst[0:2 * EXPERTS, C_IDENT:C_IDENT + 2 * EXPERTS])
                k.then_inc(S["gt"], 1)

            def up(m):
                e.wait_ge(S["lo"], KC * (m + 1))
                for f in range(FC):
                    n = FC * m + f
                    if n >= 2:
                        e.wait_ge(S["relu"], n - 1)
                    cols = slice(P * f, P * f + P)
                    for c in range(KC):
                        for k, (a, b) in enumerate(((up_hi, yT_hi), (up_hi, yT_lo), (up_lo, yT_hi))):
                            i = e.matmul((B2, B3)[n % 2], a[:, c, cols], b[m % 2][:, c, :],
                                         start=(c == 0 and k == 0), stop=(c == KC - 1 and k == 2))
                    i.then_inc(S["u"], 1)

            def down(m):
                for t in range(GROUP):
                    n = GROUP * m + t
                    toks = slice(P * t, P * t + P)
                    if n >= 2:
                        e.wait_ge(S["tot"], n - 1)
                    into = pair[:, n % 2, :]
                    route = (B6, B7)[n % 2]
                    for c in range(KC):
                        for k, (a, b) in enumerate(((yT_hi, route_hi), (yT_hi, route_lo), (yT_lo, route_hi))):
                            e.matmul(route, a[m % 2][:, c, toks], b[:, c, :],
                                     start=(c == 0 and k == 0), stop=(c == KC - 1 and k == 2))
                    for f in range(FC):
                        if t == 0:
                            e.wait_ge(S["ulo"], FC * m + f + 1)
                        for k, (a, b) in enumerate(((u_hi, down_hi), (u_hi, down_lo), (u_lo, down_hi))):
                            i = e.matmul(into, a[:, f, toks], b[:, f, :],
                                         start=(f == 0 and k == 0), stop=(f == FC - 1 and k == 2))
                    i.then_inc(S["dr"], 1)

            turn(0)
            gate_products(0)
            for m in range(GROUPS):
                up(m)
                turn_gates(m)
                if m + 1 < GROUPS:
                    turn(m + 1)
                    gate_products(m + 1)
                down(m)

        @block.scalar
        def _(e):
            def high(m):
                for c in range(KC):
                    n = KC * m + c
                    e.wait_ge(S["t"], n + 1)
                    if m >= 2 and c == 0:
                        e.wait_ge(S["dr"], GROUP * (m - 1))
                    e.activation(yT_hi[m % 2][:, c, :], (B4, B5)[c % 2], ACT.Copy).then_inc(S["hi"], 1)
                e.wait_ge(S["g"], m + 1)
                if m:
                    e.wait_ge(S["gt"], m)
                e.activation(gates[:, :], B4[0:2 * EXPERTS, :], ACT.Copy).then_inc(S["gc"], 1)

            high(0)
            for m in range(GROUPS):
                for f in range(FC + 1):
                    n = FC * m + f
                    if f < FC:
                        e.wait_ge(S["u"], n + 1)
                        if n >= 3:
                            e.wait_ge(S["ulo"], n - 2)
                        e.activation(act[n % 3][:, :], (B2, B3)[n % 2], ACT.Relu).then_inc(S["relu"], 1)
                    if f:
                        e.wait_ge(S["act"], n)
                        if m and f == 1:
                            e.wait_ge(S["dr"], GROUP * m)
                        e.activation(u_hi[:, f - 1, :], act[(n - 1) % 3][:, :], ACT.Copy).then_inc(S["uhi"], 1)
                if m + 1 < GROUPS:
                    high(m + 1)
                for t in range(GROUP):
                    n = GROUP * m + t
                    e.wait_ge(S["dr"], n + 1)
                    e.wait_ge(S["w"], m + 1)
                    if n >= 2:
                        e.wait_ge(S["gam"], n - 1)
                    e.activation(total[n % 2][:, :], (B6, B7)[n % 2], ACT.Identity,
                                 scale=weight[m % 2][:, t:t + 1]).then_inc(S["route"], 1)
                    e.wait_ge(S["shift"], n + 1)
                    e.activation(total[n % 2][:, :], total[n % 2][:, :], ACT.Identity,
                                 bias=fshift[n % 2][:, 0:1], scale=frstd[n % 2][:, 0:1]) \
                        .then_inc(S["norm"], 1)

        @block.vector
        def _(e):
            def low(m):
                for c in range(KC):
                    n = KC * m + c
                    e.wait_ge(S["hi"], n + 1)
                    e.tensor_tensor(yT_lo[m % 2][:, c, :], (B4, B5)[c % 2], yT_hi[m % 2][:, c, :].bitcast(F32),
                                    ALU.subtract).then_inc(S["lo"], 1)

            low(0)
            for m in range(GROUPS):
                for f in range(FC):
                    n = FC * m + f
                    e.wait_ge(S["relu"], n + 1)
                    e.tensor_tensor(act[n % 3][:, :], act[n % 3][:, :], act[n % 3][:, :], ALU.mult) \
                        .then_inc(S["act"], 1)
                e.wait_ge(S["gt"], m + 1)
                e.tensor_copy(gates_t[:, :, :], B5[:, 0:GROUP * 2 * EXPERTS]
                              .rearrange("p (t n) -> p t n", t=GROUP)).then_inc(S["gtc"], 1)
                e.wait_ge(S["gtc"], m + 1)
                e.tensor_tensor(logits[:, :, :], gates_t[:, :, 0:EXPERTS], gates_t[:, :, EXPERTS:2 * EXPERTS],
                                ALU.add).then_inc(S["log"], 1)
                e.wait_ge(S["log"], m + 1)
                for t in range(GROUP):
                    k = e.max(best[:, t, :], logits[:, t, :])
                k.then_inc(S["best"], 1)
                e.wait_ge(S["best"], m + 1)
                e.tensor_tensor(weight[m % 2][:, :], best[:, :, 0], best[:, :, 1], ALU.add).then_inc(S["w"], 1)
                e.wait_ge(S["w"], m + 1)
                if m + 1 < GROUPS:
                    low(m + 1)
                for t in range(GROUP):
                    n = GROUP * m + t
                    b = n % 2
                    e.wait_ge(S["route"], n + 1)
                    e.tensor_tensor(total[b][:, :], total[b][:, :], pair[:, b, :], ALU.add) \
                        .then_inc(S["tot"], 1)
                    e.wait_ge(S["tot"], n + 1)
                    e.bn_stats(fstats[:, :], total[b][:, :]).then_inc(S["bn"], 1)
                    e.wait_ge(S["bn"], n + 1)
                    e.bn_aggr(fmv[b][:, :], fstats[:, :]).then_inc(S["aggr"], 1)
                    e.wait_ge(S["aggr"], n + 1)
                    e.tensor_scalar(fve[b][:, :], fmv[b][:, 1:2], EPS, None, ALU.add).then_inc(S["eps"], 1)
                    e.wait_ge(S["rstd"], n + 1)
                    e.scalar_tensor_tensor(fshift[b][:, :], fmv[b][:, 0:1], -1.0, frstd[b][:, :],
                                           ALU.mult, ALU.mult).then_inc(S["shift"], 1)
                    e.wait_ge(S["norm"], n + 1)
                    if n == 0:
                        e.wait_ge(f_ln, 16)
                    if n >= 3:
                        e.wait_ge(f_out[n % 3], 16 * (n // 3))
                    e.tensor_tensor(ot[n % 3][:, :], total[b][:, :], lnw[:, 0, :], ALU.mult) \
                        .then_inc(S["gam"], 1)
                    e.wait_ge(S["gam"], n + 1)
                    e.tensor_tensor(ot[n % 3][:, :], ot[n % 3][:, :], lnw[:, 1, :], ALU.add) \
                        .then_inc(S["bet"], 1)
                    e.wait_ge(S["bet"], n + 1)
                    e.wait_ge(f_x1[t], 16 * (m + 1))
                    e.tensor_tensor(ot[n % 3][:, :], ot[n % 3][:, :], x1g[t][:, :], ALU.add) \
                        .then_inc(S["res"], 1)

        @block.gpsimd
        def _(e):
            for m in range(GROUPS):
                for f in range(FC):
                    n = FC * m + f
                    e.wait_ge(S["uhi"], n + 1)
                    if m and f == 0:
                        e.wait_ge(S["dr"], GROUP * m)
                    e.tensor_tensor(u_lo[:, f, :], act[n % 3][:, :], u_hi[:, f, :].bitcast(F32), ALU.subtract) \
                        .then_inc(S["ulo"], 1)
                for t in range(GROUP):
                    n = GROUP * m + t
                    e.wait_ge(S["eps"], n + 1)
                    e.tensor_tensor(frstd[n % 2][:, :], fve[n % 2][:, :], cst[:, C_POW:C_POW + 1], ALU.pow) \
                        .then_inc(S["rstd"], 1)
    top.close()


def chunked(w):
    return np.ascontiguousarray(w.reshape(-1, P, w.shape[1]).transpose(1, 0, 2))


def kernel(x, itok_B_0_15, itok_B_3_7, L0_cond_weights, L0_attn_w_qkv, L0_attn_q_ln_w, L0_attn_q_ln_b,
           L0_attn_k_ln_w, L0_attn_k_ln_b, L0_attn_w_out, L0_cond2_weight, L0_ffn_gate_w, L0_ffn_up_w,
           L0_ffn_down_w, L0_ffn_fc1_w, L0_ffn_fc2_w, L0_ffn_expert_w, L0_ffn_ln_gamma, L0_ffn_ln_beta):
    import concourse.bacc as bacc
    from concourse.bass_utils import run_bass_kernel_spmd

    a = lambda v: np.asarray(v)
    side = lambda v: a(v).reshape(KC, P).T
    arrays = {
        "x": a(x).reshape(TOKENS, DM),
        "style_ids": a(itok_B_0_15).reshape(1, BATCHES),
        "adapter_ids": a(itok_B_3_7).reshape(1, BATCHES),
        "style_w": a(L0_cond_weights).reshape(STYLES * SEQ, SEQ),
        "wqkv": a(L0_attn_w_qkv).reshape(3, DM, KC, P).transpose(3, 0, 2, 1),
        "wo": a(L0_attn_w_out).reshape(DM, HG, BPT, HD).transpose(1, 3, 2, 0).reshape(P, BPT, DM),
        "qk_ln": np.concatenate([side(v) for v in (L0_attn_q_ln_w, L0_attn_q_ln_b, L0_attn_k_ln_w,
                                                   L0_attn_k_ln_b)], axis=1),
        "w2": a(L0_cond2_weight).reshape(ADAPTERS, DM, KC, P).transpose(3, 0, 2, 1),
        "w_up": chunked(a(L0_ffn_up_w)),
        "w_down": chunked(a(L0_ffn_down_w)),
        "fc1t": chunked(a(L0_ffn_fc1_w).T),
        "expert": chunked(a(L0_ffn_expert_w)),
        "fc2": chunked(a(L0_ffn_fc2_w)),
        "gate": chunked(a(L0_ffn_gate_w)),
        "ffn_ln": np.concatenate([a(L0_ffn_ln_gamma), a(L0_ffn_ln_beta)]).reshape(1, 2 * DM),
        "consts": constants(),
    }
    arrays = {n: np.ascontiguousarray(v) for n, v in arrays.items()}
    nc = bacc.Bacc("TRN2", target_bir_lowering=False, num_devices=1)
    aps = {n: nc.dram_tensor(f"in_{n}", v.shape, mybir.dt.from_np(v.dtype), kind="ExternalInput").ap()
           for n, v in arrays.items()}
    aps["out"] = nc.dram_tensor("out", (TOKENS, DM), F32, kind="ExternalOutput").ap()
    program(nc, **aps)
    r = run_bass_kernel_spmd(nc, [{f"in_{n}": v for n, v in arrays.items()}], core_ids=[0])
    return r.results[0]["out"].reshape(BATCHES, SEQ, DM)
```

```python
from contextlib import ExitStack

import numpy as np

import concourse.bass as bass
from concourse import mybir

F32 = mybir.dt.float32
F32R = mybir.dt.float32r
BF16 = mybir.dt.bfloat16
I32 = mybir.dt.int32
ALU = mybir.AluOpType
ACT = mybir.ActivationFunctionType
AX = mybir.AxisListType

P = 128
BATCHES, SEQ, DM = 128, 32, 512
TOKENS = BATCHES * SEQ
BPT = P // SEQ
TILES = TOKENS // P
KC = DM // P
HEADS, HD = 32, 16
HPC = P // HD
HG = HEADS // BPT
STYLES = 16
ADAPTERS = 8
SLOTS = (BATCHES + ADAPTERS * (BPT - 1)) // BPT
INNER = 1024
FC = INNER // P
LAT = 256
LC = LAT // P
EXPERTS = 8
GROUP = 4
GROUPS = TILES // GROUP
CLIP = 8.0
SCALE = HD ** -0.5
EPS = 1e-5
MASKED = -1e30
ABSENT = 2.0 ** 17

C_BIAS = 0
C_IDENT = C_BIAS + HEADS * SEQ
C_KMASK = C_IDENT + P
C_VMASK = C_KMASK + HPC * SEQ
VW = BPT * HD + BPT
C_WMASK = C_VMASK + VW
C_ROW = C_WMASK + P
C_SLOT = C_ROW + P
C_VAL = C_SLOT + SLOTS * BPT
C_COL = C_VAL + SEQ
C_PMOD = C_COL + 1
C_POW = C_PMOD + 1
C_SIZE = C_POW + 2


def constants():
    p = np.arange(P)
    q = p % SEQ
    c = np.zeros((P, C_SIZE), np.float32)
    m = np.arange(1, HEADS + 1, dtype=np.float32) * np.float32(8 / HEADS)
    slopes = (np.float32(1.0) / np.power(np.float32(2.0), m)).astype(np.float32)
    rel = (np.arange(SEQ)[None, :] - q[:, None]).astype(np.float32)
    bias = slopes[None, :, None] * rel[:, None, :]
    c[:, C_BIAS:C_IDENT] = np.where(rel[:, None, :] <= 0, bias, np.float32(MASKED)).reshape(P, -1)
    c[:, C_IDENT:C_KMASK] = np.eye(P)
    c[:, C_KMASK:C_VMASK] = np.repeat(p[:, None] // HD == np.arange(HPC)[None, :], SEQ, axis=1)
    own = p[:, None] // SEQ == np.arange(BPT)[None, :]
    c[:, C_VMASK:C_VMASK + BPT * HD] = np.repeat(own, HD, axis=1)
    c[:, C_VMASK + BPT * HD:C_WMASK] = own
    c[:, C_WMASK:C_ROW] = np.repeat(own, SEQ, axis=1)
    c[:, C_ROW:C_SLOT] = p[None, :]
    c[:, C_SLOT:C_VAL] = np.arange(SLOTS * BPT)[None, :]
    c[:, C_VAL:C_COL] = (SEQ * p - ABSENT)[:, None]
    c[:, C_COL] = p
    c[:, C_PMOD] = q
    c[:, C_POW:C_POW + 2] = -0.5
    return c


def program(nc, x, style_ids, adapter_ids, style_w, wqkv, wo, qk_ln, w2, w_up, w_down, fc1t, expert,
            fc2, gate, ffn_ln, consts, out):
    x1_rows = nc.dram_tensor("x1_rows", [TOKENS, DM], F32, kind="Internal").ap()
    y_rows = nc.dram_tensor("y_rows", [TOKENS, DM], F32, kind="Internal").ap()
    top = ExitStack()

    def tiles_in(stack):
        def sb(name, shape, dt=F32):
            return stack.enter_context(nc.sbuf_tensor(name, shape, dt))
        return sb

    sb = tiles_in(top)

    def psum(name, shape, dt=F32):
        return top.enter_context(nc.psum_tensor(name, shape, dt))

    def sem(name):
        return top.enter_context(nc.semaphore(name))

    cst = sb("cst", [P, C_SIZE])
    ident = cst[:, C_IDENT:C_KMASK]
    bias = cst[:, C_BIAS:C_IDENT].rearrange("p (h k) -> p h k", h=HEADS)
    kmask = sb("kmask", [P, HPC * SEQ], BF16)
    vmask = sb("vmask", [P, VW], BF16)
    qkln = sb("qkln", [P, 4 * KC])
    slot_rows = sb("slot_rows", [P, SLOTS], I32)
    slot_adapter = sb("slot_adapter", [1, SLOTS], I32)
    bank = [psum(f"bank{i}", [P, DM]) for i in range(2, 8)]
    pair = psum("pair", [P, 2, DM])
    B2, B3, B4, B5, B6, B7 = (b[:, :] for b in bank)

    tile_rows = sb("tile_rows", [P, TILES], I32)
    style_idx = sb("style_idx", [P, TILES], I32)
    w2t = [sb(f"w2t{i}", [P, KC, DM]) for i in range(2)]
    xg = [sb(f"xg{i}", [P, DM]) for i in range(2)]
    xgT = sb("xgT", [P, DM])
    ys = [sb(f"ys{i}", [P, DM]) for i in range(2)]

    weights = ExitStack()
    wsb = tiles_in(weights)
    wqkv_hi = wsb("wqkv_hi", [P, 3, KC, DM], F32R)
    wqkv_lo = wsb("wqkv_lo", [P, 3, KC, DM], F32R)
    wo_hi = wsb("wo_hi", [P, BPT, DM], F32R)
    wo_lo = wsb("wo_lo", [P, BPT, DM], F32R)

    XR, VR = 8, 5
    att = ExitStack()
    asb = tiles_in(att)
    xt = [asb(f"xt{i}", [P, DM]) for i in range(XR)]
    style_rows = [asb(f"style_rows{i}", [P, SEQ]) for i in range(XR)]
    style_bd = [asb(f"style_bd{i}", [P, BPT, SEQ]) for i in range(2)]
    h_hi = [asb(f"h_hi{i}", [P, KC, P], F32R) for i in range(2)]
    h_lo = [asb(f"h_lo{i}", [P, KC, P], F32R) for i in range(2)]
    qn = [asb(f"qn{i}", [P, DM]) for i in range(2)]
    kn = [asb(f"kn{i}", [P, DM]) for i in range(2)]
    stats = [asb(f"stats{i}", [P, 2, 6]) for i in range(2)]
    mean_var = [asb(f"mean_var{i}", [P, 2, 2]) for i in range(2)]
    var_eps = [asb(f"var_eps{i}", [P, 2]) for i in range(2)]
    rstd = [asb(f"rstd{i}", [P, 2]) for i in range(2)]
    shift = [asb(f"shift{i}", [P, 2]) for i in range(2)]
    qT = asb("qT", [P, KC, P])
    kT = asb("kT", [P, KC, P])
    q_hi = asb("q_hi", [P, KC, P], BF16)
    k_hi = asb("k_hi", [P, KC * P], BF16)
    v_hi = [asb(f"v_hi{i}", [P, HEADS, HD], BF16) for i in range(VR)]
    v_lo = [asb(f"v_lo{i}", [P, HEADS, HD], BF16) for i in range(VR)]
    p_hi = asb("p_hi", [P, HEADS * SEQ], BF16)
    p_lo = asb("p_lo", [P, HEADS * SEQ], BF16)
    o_hi = asb("o_hi", [P, BPT, P], F32R)
    o_lo = asb("o_lo", [P, BPT, P], F32R)
    x1t = [asb(f"x1t{i}", [P, DM]) for i in range(2)]

    prep = ExitStack()
    psb = tiles_in(prep)
    stage = [psb(f"stage{i}", [P, KC, DM]) for i in range(4)]
    ids_row = psb("ids_row", [P, BATCHES], I32)
    ids_col = psb("ids_col", [P, 1], I32)
    style_col = psb("style_col", [P, 1], I32)
    idr = psb("idr", [P, BATCHES])
    idc = psb("idc", [P, 1])
    stylec = psb("stylec", [P, 1])
    keyr = psb("keyr", [P, BATCHES])
    keyc = psb("keyc", [P, 1])
    before = psb("before", [P, BATCHES])
    after = psb("after", [P, BATCHES])
    same = psb("same", [P, BATCHES])
    rank = psb("rank", [P, 1])
    sorted_row = psb("sorted_row", [P, 1])
    at_rank = psb("at_rank", [P, BATCHES])
    style_of = psb("style_of", [P, SEQ])
    row_of = psb("row_of", [P, SEQ])
    within = psb("within", [P, 1])
    within_i = psb("within_i", [P, 1], I32)
    place_i = psb("place_i", [P, 1], I32)
    place = psb("place", [P, 1])
    first = psb("first", [P, 1])
    earlier = psb("earlier", [P, 1])
    slot_no = psb("slot_no", [P, 1])
    column = psb("column", [P, 1])
    onehot = psb("onehot", [P, SLOTS * BPT])
    scaled = psb("scaled", [P, TILES])
    table_f = [psb(f"table_f{i}", [P, SLOTS]) for i in range(4)]
    prep.close()

    kx_hi = asb("kx_hi", [P, KC * BPT, HPC, SEQ], BF16)
    kx_lo = asb("kx_lo", [P, KC * BPT, HPC, SEQ], BF16)
    vx_hi = asb("vx_hi", [P, HEADS, VW], BF16)
    vx_lo = asb("vx_lo", [P, HEADS, VW], BF16)
    probs = asb("probs", [P, HEADS, SEQ])
    probsT = asb("probsT", [P, HEADS * SEQ])
    on = asb("on", [P, BPT, HG, HD])
    row_max = asb("row_max", [P, HEADS])
    recip = asb("recip", [P, 2, 4, BPT])
    vf = [asb(f"vf{i}", [P, DM]) for i in range(2)]
    k_lo = asb("k_lo", [P, KC * P], BF16)
    q_lo = asb("q_lo", [P, KC, P], BF16)

    s_cst, s_ids = sem("s_cst"), sem("s_ids")
    s_stage = [sem(f"s_stage{i}") for i in range(4)]
    s_whi, s_wlo = sem("s_whi"), sem("s_wlo")
    s_t = sem("s_t")
    s_tp = sem("s_tp")
    s_tables = sem("s_tables")
    STEP_ROW_OF, STEP_FIRST, STEP_ONEHOT = 14, 20, 24

    a_x = [sem(f"a_load{i}") for i in range(XR)]
    a_store = [sem(f"a_store{i}") for i in range(2)]
    names = ("style", "h", "hhi", "hlo", "pq", "pk", "pv", "cq", "ck", "bn", "aggr", "eps", "rstd", "shift",
             "qn", "kn", "tq", "tk", "qT", "kT", "qhi", "qlo", "khi", "klo", "kxhi", "kxlo", "cv", "vhi",
             "vlo", "vxhi", "vxlo", "vx1", "s", "sb", "max", "sub", "exp", "pT", "phi", "plo", "o", "rec",
             "on", "ot", "ohi", "olo", "r", "x1", "mask")
    A = {n: sem(f"a_{n}") for n in names}
    PER = {"bn": 2, "sb": 2, "on": 2}
    T = TILES
    LAG = 6
    STEPS = SLOTS + LAG

    def upto(e, name, i):
        if i >= 0:
            e.wait_ge(A[name], PER.get(name, 1) * (i + 1))

    att.close()
    weights.close()

    up_hi = sb("up_hi", [P, KC, INNER], F32R)
    up_lo = sb("up_lo", [P, KC, INNER], F32R)
    down_hi = sb("down_hi", [P, FC, DM], F32R)
    down_lo = sb("down_lo", [P, FC, DM], F32R)
    route_hi = sb("route_hi", [P, KC, DM], F32R)
    route_lo = sb("route_lo", [P, KC, DM], F32R)
    gate_hl = sb("gate_hl", [P, KC, 2, EXPERTS], F32R)
    make = ExitStack()
    msb = tiles_in(make)
    raw = [msb(f"raw{i}", [P, KC, DM]) for i in range(2)]
    gate_raw = msb("gate_raw", [P, KC, EXPERTS])
    fc1_sb = msb("fc1_sb", [P, LC, DM])
    ex_sb = msb("ex_sb", [P, LC, LAT])
    fc2_sb = msb("fc2_sb", [P, LC, DM])
    latT = msb("latT", [P, LC, DM])
    make.close()
    m_raw, m_fc = [sem("m_raw0"), sem("m_raw1")], sem("m_fc")
    m_hi, m_lo, m_lat, m_latc, m_route = sem("m_hi"), sem("m_lo"), sem("m_lat"), sem("m_latc"), sem("m_route")
    d_zero, d_w2, d_x = sem("d_zero"), [sem("d_w20"), sem("d_w21")], [sem("d_x0"), sem("d_x1")]
    d_y = [sem("d_y0"), sem("d_y1")]
    d_t, d_tc, d_m, d_mc = sem("d_t"), sem("d_tc"), sem("d_m"), sem("d_mc")
    pieces = [(w_up[:, :, DM * n:DM * n + DM], up_hi[:, :, DM * n:DM * n + DM],
               up_lo[:, :, DM * n:DM * n + DM]) for n in range(INNER // DM)]
    pieces += [(w_down[:, KC * n:KC * n + KC, :], down_hi[:, KC * n:KC * n + KC, :],
                down_lo[:, KC * n:KC * n + KC, :]) for n in range(FC // KC)]
    PC = len(pieces)


    def made_in(i):
        n = i - (T + 4)
        if n < 0:
            return []
        if i == STEPS - 1:
            return range(n, PC + KC + 1)
        return [n] if n < PC + KC + 1 else []

    with nc.Block() as block:
        @block.sync
        def _(e):
            e.dma_start(cst[:, :], consts).then_inc(s_cst, 16)
            for dst, src in ((ids_row[:, :], adapter_ids.broadcast_to([P, BATCHES])),
                             (ids_col[:, :], adapter_ids.rearrange("o b -> b o")),
                             (style_col[:, :], style_ids.rearrange("o b -> b o")),
                             (qkln[:, :], qk_ln)):
                e.dma_start(dst, src).then_inc(s_ids, 16)
            for n in range(4):
                e.dma_start(stage[n][:, :, :], wqkv[:, n] if n < 3 else wo).then_inc(s_stage[n], 16)
            e.wait_ge(s_tables, 2)
            for i in range(STEPS):
                t = i - 5
                if 0 <= t < T:
                    upto(e, "x1", t)
                    e.dma_start(x1_rows[P * t:P * t + P, :], x1t[t % 2][:, :]).then_inc(a_store[t % 2], 16)
                s = i - LAG + 1
                if 0 <= s < SLOTS:
                    if s >= 2:
                        e.wait_ge(d_m, s - 1)
                    adapter = e.value_load(slot_adapter[0:1, s:s + 1], min_val=0, max_val=ADAPTERS - 1)
                    e.dma_start(w2t[s % 2][:, :, :].rearrange("p (o c) n -> p o (c n)", o=1),
                                w2[:, bass.ds(adapter, 1), :]).then_inc(d_w2[s % 2], 16)
                if t == T - 1:
                    for dst, src in ((fc1_sb, fc1t), (ex_sb, expert), (fc2_sb, fc2), (gate_raw, gate)):
                        e.dma_start(dst[:, :, :], src).then_inc(m_fc, 16)
                if t >= T - 1:
                    for n in range(*((0, 2) if t == T - 1 else (t - T + 2, t - T + 3))):
                        if n < PC:
                            if n >= 2:
                                e.wait_ge(m_lo, n - 1)
                            e.dma_start(raw[n % 2][:, :, :], pieces[n][0]).then_inc(m_raw[n % 2], 16)

        @block.tensor
        def _(e):
            def style(t):
                e.wait_ge(a_x[t % XR], 32 * (t // XR + 1))
                upto(e, "style", t)
                if t > LAG + 1:
                    e.wait_ge(d_tc, t - LAG - 1)
                upto(e, "hlo", t - 1)
                for c in range(KC):
                    m = e.matmul(B7[:, P * c:P * c + P], xt[t % XR][:, P * c:P * c + P],
                                 style_bd[t % 2][:, :, :].rearrange("p j d -> p (j d)"), start=True, stop=True)
                m.then_inc(A["h"], 1)

            def project(t, n, into, name):
                upto(e, "hlo", t)
                e.wait_ge(s_wlo, n + 1)
                hi, lo = h_hi[t % 2], h_lo[t % 2]
                for c in range(KC):
                    for k, (a, b) in enumerate(((hi, wqkv_hi), (hi, wqkv_lo), (lo, wqkv_hi))):
                        m = e.matmul(into, a[:, c, :], b[:, n, c, :], start=(c == 0 and k == 0),
                                     stop=(c == KC - 1 and k == 2))
                m.then_inc(A[name], 1)

            def values(t):
                upto(e, "phi", t)
                upto(e, "plo", t)
                upto(e, "vxlo", t)
                e.wait_ge(A["vx1"], 1)
                upto(e, "sb", min(t + 1, T - 1))
                for g in range(HG):
                    dst = pair[:, g // 4, VW * (g % 4):VW * (g % 4) + VW]
                    for k, (a, b, w) in enumerate(((p_hi, vx_hi, VW), (p_lo, vx_hi, VW),
                                                   (p_hi, vx_lo, BPT * HD))):
                        for j in range(BPT):
                            h = BPT * g + j
                            m = e.matmul(dst[SEQ * j:SEQ * j + SEQ, 0:w], a[:, SEQ * h:SEQ * h + SEQ],
                                         b[:, h, 0:w], start=(k == 0), stop=(k == 2),
                                         skip_group_check=True)
                m.then_inc(A["o"], 1)

            def turn_values(t):
                upto(e, "on", t)
                upto(e, "olo", t - 1)
                if t + 4 - LAG > 0:
                    e.wait_ge(d_mc, t + 4 - LAG)
                for b in range(BPT):
                    m = e.transpose(B4[:, P * b:P * b + P],
                                    on[:, b, :, :].rearrange("p g d -> p (g d)"), ident)
                m.then_inc(A["ot"], 1)

            def out_project(t):
                upto(e, "olo", t)
                e.wait_ge(s_wlo, 4)
                upto(e, "x1", t - 1)
                for j in range(BPT):
                    for k, (a, b) in enumerate(((o_hi, wo_hi), (o_hi, wo_lo), (o_lo, wo_hi))):
                        m = e.matmul(B6, a[:, j, :], b[:, j, :], start=(j == 0 and k == 0),
                                     stop=(j == BPT - 1 and k == 2))
                m.then_inc(A["r"], 1)

            def turn(t, src, done, into, name):
                upto(e, done, t)
                for c in range(KC):
                    m = e.transpose(into[:, P * c:P * c + P], src[:, P * c:P * c + P], ident)
                m.then_inc(A[name], 1)

            def scores(t):
                for n in ("qhi", "qlo", "kxhi", "kxlo"):
                    upto(e, n, t)
                upto(e, "on", t - 2)
                for c in range(KC):
                    dst = pair[:, c // 2, 256 * (c % 2):256 * (c % 2) + 256]
                    for k, (a, b) in enumerate(((q_hi, kx_hi), (q_lo, kx_hi), (q_hi, kx_lo))):
                        for j in range(BPT):
                            m = e.matmul(dst[SEQ * j:SEQ * j + SEQ, :], a[:, c, SEQ * j:SEQ * j + SEQ],
                                         b[:, BPT * c + j, :, :].rearrange("p h k -> p (h k)"),
                                         start=(k == 0), stop=(k == 2), skip_group_check=True)
                m.then_inc(A["s"], 1)

            def turn_slot(s):
                e.wait_ge(d_x[s % 2], 16 * (s // 2 + 1))
                upto(e, "hlo", min(s + LAG + 1, T - 1))
                if s >= 1:
                    e.wait_ge(d_tc, s)
                for c in range(KC):
                    m = e.transpose(B7[:, P * c:P * c + P], xg[s % 2][:, P * c:P * c + P], ident)
                m.then_inc(d_t, 1)

            def adapt_slot(s):
                e.wait_ge(d_tc, s + 1)
                e.wait_ge(d_w2[s % 2], 16 * (s // 2 + 1))
                upto(e, "olo", min(s + LAG - 4, T - 1))
                if s >= 1:
                    e.wait_ge(d_mc, s)
                for c in range(KC):
                    m = e.matmul(B4, xgT[:, P * c:P * c + P], w2t[s % 2][:, c, :],
                                 start=(c == 0), stop=(c == KC - 1))
                m.then_inc(d_m, 1)

            def make_route(i):
                if i == T + 5:
                    e.wait_ge(m_fc, 64)
                    for m_ in range(LC):
                        for k in range(LC):
                            m = e.matmul((B5, B6)[m_], ex_sb[:, k, P * m_:P * m_ + P], fc1_sb[:, k, :],
                                         start=(k == 0), stop=(k == LC - 1))
                        m.then_inc(m_lat, 1)
                c = i - (T + 6)
                if 0 <= c < KC:
                    e.wait_ge(m_latc, LC)
                    if c >= 2:
                        e.wait_ge(m_lo, PC + c - 1)
                    for k in range(LC):
                        m = e.matmul((B5, B6)[c % 2], latT[:, k, P * c:P * c + P], fc2_sb[:, k, :],
                                     start=(k == 0), stop=(k == LC - 1))
                    m.then_inc(m_route, 1)

            e.wait_ge(s_t, STEP_ROW_OF)
            for j in range(BPT):
                q = slice(SEQ * j, SEQ * j + SEQ)
                e.matmul(B2[q, 0:TILES], cst[:, C_VAL:C_COL], at_rank[:, j::BPT], start=True, stop=True)
                m = e.matmul(B3[q, 0:TILES], style_of[:, :], at_rank[:, j::BPT], start=True, stop=True)
            m.then_inc(s_tp, 1)
            e.wait_ge(s_t, STEP_FIRST)
            e.matmul(B4[:, 0:1], after[:, :], first[:, :], start=True, stop=True).then_inc(s_tp, 1)
            e.wait_ge(s_t, STEP_ONEHOT)
            for j in range(BPT):
                e.matmul(B5[SEQ * j:SEQ * j + SEQ, 0:SLOTS], row_of[:, :], onehot[:, j::BPT],
                         start=True, stop=True)
            e.matmul(B6[0:1, 0:SLOTS], idc[:, :], onehot[:, 0::BPT], start=True, stop=True) \
                .then_inc(s_tp, 1)
            e.wait_ge(s_tables, 2)

            style(0)
            for i in range(STEPS):
                live = lambda t: 0 <= t < T
                slot = 0 <= i - LAG < SLOTS
                if i + 1 < T:
                    style(i + 1)
                if live(i):
                    upto(e, "cq", i - 1)
                    project(i, 0, B2, "pq")
                if live(i - 4):
                    values(i - 4)
                if live(i):
                    upto(e, "ck", i - 1)
                    upto(e, "qT", i - 2)
                    project(i, 1, B3, "pk")
                if live(i - 4):
                    turn_values(i - 4)
                if live(i):
                    upto(e, "cv", i - 1)
                    upto(e, "kT", i - 2)
                    project(i, 2, B5, "pv")
                if slot:
                    turn_slot(i - LAG)
                if live(i - 4):
                    out_project(i - 4)
                if live(i - 1):
                    upto(e, "ck", min(i, T - 1))
                    turn(i - 1, qn[(i - 1) % 2], "qn", B3, "tq")
                    upto(e, "cv", min(i, T - 1))
                    turn(i - 1, kn[(i - 1) % 2], "kn", B5, "tk")
                if slot:
                    adapt_slot(i - LAG)
                make_route(i)
                if live(i - 2):
                    scores(i - 2)

        @block.scalar
        def _(e):
            def high(n):
                if n < PC:
                    e.wait_ge(m_raw[n % 2], 16 * (n // 2 + 1))
                    e.activation(pieces[n][1], raw[n % 2][:, :, :], ACT.Copy).then_inc(m_hi, 1)
                elif n < PC + KC:
                    e.wait_ge(m_route, n - PC + 1)
                    e.activation(route_hi[:, n - PC, :], (B5, B6)[(n - PC) % 2], ACT.Copy).then_inc(m_hi, 1)
                elif n == PC + KC:
                    e.wait_ge(m_fc, 64)
                    e.activation(gate_hl[:, :, 0, :], gate_raw[:, :, :], ACT.Copy).then_inc(m_hi, 1)

            for n in range(4):
                e.wait_ge(s_stage[n], 16)
                dst = wqkv_hi[:, n] if n < 3 else wo_hi[:, :, :]
                e.activation(dst, stage[n][:, :, :], ACT.Copy).then_inc(s_whi, 1)
            for i in range(-1, STEPS):
                live = lambda t: 0 <= t < T
                t = i - 2
                if live(t):
                    upto(e, "tq", t)
                    upto(e, "qlo", t - 1)
                    for c in range(KC):
                        m = e.activation(qT[:, c, :], B3[:, P * c:P * c + P], ACT.Identity,
                                         bias=qkln[:, KC + c:KC + c + 1], scale=qkln[:, c:c + 1])
                    m.then_inc(A["qT"], 1)
                if live(i + 1):
                    t = i + 1
                    upto(e, "h", t)
                    upto(e, "pv", t - 2)
                    e.activation(h_hi[t % 2][:, :, :], B7.rearrange("p (c t) -> p c t", c=KC), ACT.Copy) \
                        .then_inc(A["hhi"], 1)
                t = i - 2
                if live(t):
                    upto(e, "tk", t)
                    upto(e, "klo", t - 1)
                    for c in range(KC):
                        m = e.activation(kT[:, c, :], B5[:, P * c:P * c + P], ACT.Identity,
                                         bias=qkln[:, 3 * KC + c:3 * KC + c + 1],
                                         scale=qkln[:, 2 * KC + c:2 * KC + c + 1])
                    m.then_inc(A["kT"], 1)
                    upto(e, "kT", t)
                    upto(e, "kxlo", t - 1)
                    e.activation(k_hi[:, :], kT[:, :, :].rearrange("p c t -> p (c t)"), ACT.Copy) \
                        .then_inc(A["khi"], 1)
                    upto(e, "qT", t)
                    upto(e, "s", t - 1)
                    e.activation(q_hi[:, :, :], qT[:, :, :], ACT.Copy).then_inc(A["qhi"], 1)
                t = i - 3
                if live(t):
                    upto(e, "sub", t)
                    e.activation(probs[:, :, :], probs[:, :, :], ACT.Exp).then_inc(A["exp"], 1)
                    upto(e, "pT", t)
                    upto(e, "o", t - 1)
                    e.activation(p_hi[:, :], probsT[:, :], ACT.Copy).then_inc(A["phi"], 1)
                t = i - 4
                if live(t):
                    upto(e, "ot", t)
                    upto(e, "r", t - 1)
                    e.activation(o_hi[:, :, :].rearrange("p j (b q) -> p j b q", b=BPT),
                                 B4.rearrange("p (b j q) -> p j b q", b=BPT, j=BPT), ACT.Copy) \
                        .then_inc(A["ohi"], 1)
                s = i - LAG
                if 0 <= s < SLOTS:
                    e.wait_ge(d_t, s + 1)
                    if s >= 1:
                        e.wait_ge(d_m, s)
                    e.activation(xgT[:, :], B7, ACT.Copy).then_inc(d_tc, 1)
                if live(i):
                    t = i
                    upto(e, "shift", t)
                    for n, buf in enumerate((qn, kn)):
                        b = buf[t % 2]
                        e.activation(b[:, :], b[:, :], ACT.Identity, bias=shift[t % 2][:, n:n + 1],
                                     scale=rstd[t % 2][:, n:n + 1]).then_inc(A[("qn", "kn")[n]], 1)
                    upto(e, "cv", t)
                    upto(e, "vxhi", t - VR)
                    e.activation(v_hi[t % VR][:, :, :], vf[t % 2][:, :].rearrange("p (h d) -> p h d", h=HEADS),
                                 ACT.Copy).then_inc(A["vhi"], 1)
                s = i - LAG
                if 0 <= s < SLOTS:
                    e.wait_ge(d_m, s + 1)
                    if s >= 2:
                        e.wait_ge(d_y[s % 2], 16 * (s // 2))
                    e.activation(ys[s % 2][:, :], B4, ACT.Copy).then_inc(d_mc, 1)
                if i == T + 5:
                    e.wait_ge(m_lat, LC)
                    for m_ in range(LC):
                        m = e.activation(latT[:, m_, :], (B5, B6)[m_], ACT.Copy)
                    m.then_inc(m_latc, LC)
                for n in made_in(i):
                    high(n)

        @block.vector
        def _(e):
            def clip(t, src, dst, name):
                e.tensor_scalar(dst, src, CLIP, -CLIP, ALU.min, ALU.max).then_inc(A[name], 1)

            def low(n):
                e.wait_ge(m_hi, n + 1)
                if n < PC:
                    dst, src, hi = pieces[n][2], raw[n % 2][:, :, :], pieces[n][1]
                elif n < PC + KC:
                    dst, src, hi = route_lo[:, n - PC, :], (B5, B6)[(n - PC) % 2], route_hi[:, n - PC, :]
                else:
                    dst, src, hi = gate_hl[:, :, 1, :], gate_raw[:, :, :], gate_hl[:, :, 0, :]
                e.tensor_tensor(dst, src, hi.bitcast(F32), ALU.subtract).then_inc(m_lo, 1)

            steps = [0]

            def step(i):
                i.then_inc(s_t, 1)
                steps[0] += 1
                e.wait_ge(s_t, steps[0])

            e.wait_ge(s_cst, 16)
            e.wait_ge(s_ids, 64)
            row, col, pmod = cst[:, C_ROW:C_SLOT], cst[:, C_COL:C_COL + 1], cst[:, C_PMOD:C_PMOD + 1]
            step(e.tensor_copy(idr[:, :], ids_row[:, :]))
            step(e.tensor_copy(idc[:, :], ids_col[:, :]))
            step(e.tensor_copy(stylec[:, :], style_col[:, :]))
            step(e.scalar_tensor_tensor(keyr[:, :], idr[:, :], float(BATCHES), row, ALU.mult, ALU.add))
            step(e.scalar_tensor_tensor(keyc[:, :], idc[:, :], float(BATCHES), col, ALU.mult, ALU.add))
            step(e.tensor_scalar(before[:, :], keyr[:, :], keyc[:, 0:1], None, ALU.is_lt))
            step(e.tensor_reduce(rank[:, :], before[:, :], AX.X, ALU.add))
            step(e.tensor_scalar(at_rank[:, :], row, rank[:, 0:1], None, ALU.is_equal))
            spread = cst[:, C_VAL:C_COL]
            step(e.tensor_scalar(style_of[:, :], spread, 0.0, stylec[:, 0:1], ALU.mult, ALU.add))
            step(e.tensor_scalar(sorted_row[:, :], rank[:, :], float(SEQ), -ABSENT, ALU.mult, ALU.add))
            step(e.tensor_scalar(row_of[:, :], spread, 0.0, sorted_row[:, 0:1], ALU.mult, ALU.add))
            step(e.tensor_scalar(after[:, :], keyr[:, :], keyc[:, 0:1], None, ALU.is_gt))
            step(e.tensor_scalar(same[:, :], idr[:, :], idc[:, 0:1], None, ALU.is_equal))
            step(e.tensor_tensor(same[:, :], same[:, :], before[:, :], ALU.mult))
            assert steps[0] == STEP_ROW_OF
            step(e.tensor_reduce(within[:, :], same[:, :], AX.X, ALU.add))
            step(e.tensor_copy(within_i[:, :], within[:, :]))
            step(e.tensor_scalar(place_i[:, :], within_i[:, :], BPT - 1, None, ALU.bitwise_and))
            step(e.tensor_copy(place[:, :], place_i[:, :]))
            step(e.tensor_scalar(first[:, :], place[:, :], 0.0, None, ALU.is_equal))
            e.wait_ge(s_tp, 1)
            step(e.tensor_scalar(table_f[0][:, 0:TILES], B2[:, 0:TILES], ABSENT, pmod, ALU.add, ALU.add))
            assert steps[0] == STEP_FIRST
            step(e.tensor_scalar(table_f[1][:, 0:TILES], B3[:, 0:TILES], float(SEQ), pmod, ALU.mult, ALU.add))
            e.tensor_copy(tile_rows[:, :], table_f[0][:, 0:TILES])
            e.tensor_copy(style_idx[:, :], table_f[1][:, 0:TILES]).then_inc(s_tables, 1)
            e.wait_ge(s_tp, 2)
            step(e.scalar_tensor_tensor(slot_no[:, :], B4[:, 0:1], -1.0, first[:, :], ALU.add, ALU.add))
            step(e.scalar_tensor_tensor(column[:, :], slot_no[:, :], float(BPT), place[:, :],
                                        ALU.mult, ALU.add))
            step(e.tensor_scalar(onehot[:, :], cst[:, C_SLOT:C_VAL], column[:, 0:1], None, ALU.is_equal))
            assert steps[0] == STEP_ONEHOT
            e.wait_ge(s_tp, 3)
            step(e.tensor_scalar(table_f[2][:, :], B5[:, 0:SLOTS], ABSENT, pmod, ALU.add, ALU.add))
            step(e.tensor_copy(table_f[3][0:1, :], B6[0:1, 0:SLOTS]))
            step(e.tensor_copy(slot_rows[:, :], table_f[2][:, :]))
            e.tensor_copy(slot_adapter[:, :], table_f[3][0:1, :]).then_inc(s_tables, 1)
            e.tensor_copy(kmask[:, :], cst[:, C_KMASK:C_VMASK]).then_inc(A["mask"], 1)
            e.tensor_copy(vmask[:, :], cst[:, C_VMASK:C_WMASK]).then_inc(A["mask"], 1)
            for n in range(4):
                e.wait_ge(s_whi, n + 1)
                hi, dst = (wqkv_hi[:, n], wqkv_lo[:, n]) if n < 3 else (wo_hi[:, :, :], wo_lo[:, :, :])
                e.tensor_tensor(dst, stage[n][:, :, :], hi.bitcast(F32), ALU.subtract).then_inc(s_wlo, 1)
            e.wait_ge(s_wlo, 4)
            e.wait_ge(s_tables, 2)
            e.wait_ge(A["mask"], 2)
            e.tensor_copy(vx_hi[:, :, BPT * HD:VW], vmask[:, BPT * HD:VW].rearrange("p (o b) -> p o b", o=1)
                          .broadcast_to([P, HEADS, BPT])).then_inc(A["vx1"], 1)
            for i in range(-1, STEPS):
                live = lambda t: 0 <= t < T
                t = i - 3
                if live(t):
                    upto(e, "s", t)
                    upto(e, "pT", t - 1)
                    for n in range(2):
                        h = slice(16 * n, 16 * n + 16)
                        e.scalar_tensor_tensor(probs[:, h, :], pair[:, n, :].rearrange("p (h k) -> p h k", k=SEQ),
                                               SCALE, bias[:, h, :], ALU.mult, ALU.add).then_inc(A["sb"], 1)
                if live(i + 1):
                    t = i + 1
                    upto(e, "hhi", t)
                    upto(e, "pv", t - 2)
                    e.tensor_tensor(h_lo[t % 2][:, :, :], B7.rearrange("p (c t) -> p c t", c=KC),
                                    h_hi[t % 2][:, :, :].bitcast(F32), ALU.subtract).then_inc(A["hlo"], 1)
                t = i - 3
                if live(t):
                    upto(e, "sb", t)
                    upto(e, "sub", t - 1)
                    e.tensor_reduce(row_max[:, :], probs[:, :, :], AX.X, ALU.max).then_inc(A["max"], 1)
                if live(i):
                    t = i
                    upto(e, "pq", t)
                    upto(e, "tq", t - 2)
                    clip(t, B2, qn[t % 2][:, :], "cq")
                    upto(e, "cq", t)
                    e.bn_stats(stats[t % 2][:, 0, :], qn[t % 2][:, :]).then_inc(A["bn"], 1)
                t = i - 4
                if live(t):
                    upto(e, "o", t)
                    o4 = pair[:, :, 0:4 * VW].rearrange("p n (g v) -> p n g v", g=4)
                    e.reciprocal(recip[:, :, :, :], o4[:, :, :, BPT * HD:VW]).then_inc(A["rec"], 1)
                    upto(e, "rec", t)
                    upto(e, "ot", t - 1)
                    for n in range(2):
                        e.tensor_tensor(on[:, :, 4 * n:4 * n + 4, :].rearrange("p b g d -> p g b d"),
                                        o4[:, n, :, 0:BPT * HD].rearrange("p g (b d) -> p g b d", b=BPT),
                                        recip[:, n, :, :].rearrange("p g (b o) -> p g b o", o=1)
                                        .broadcast_to([P, 4, BPT, HD]), ALU.mult).then_inc(A["on"], 1)
                t = i - 3
                if live(t):
                    upto(e, "exp", t)
                    upto(e, "plo", t - 1)
                    e.transpose(probsT[:, :], probs[:, :, :].rearrange("p h k -> p (h k)")) \
                        .then_inc(A["pT"], 1)
                t = i - 2
                if live(t):
                    upto(e, "khi", t)
                    upto(e, "s", t - 1)
                    wide = lambda a: a[:, :].rearrange("p (n o k) -> p n o k", o=1, k=SEQ) \
                        .broadcast_to([P, KC * BPT, HPC, SEQ])
                    mask = kmask[:, :].rearrange("p (o h k) -> p o h k", o=1, h=HPC) \
                        .broadcast_to([P, KC * BPT, HPC, SEQ])
                    e.tensor_tensor(kx_hi[:, :, :, :], wide(k_hi), mask, ALU.mult).then_inc(A["kxhi"], 1)
                t = i - 4
                if live(t):
                    upto(e, "ohi", t)
                    upto(e, "r", t - 1)
                    e.tensor_tensor(o_lo[:, :, :].rearrange("p j (b q) -> p j b q", b=BPT),
                                    B4.rearrange("p (b j q) -> p j b q", b=BPT, j=BPT),
                                    o_hi[:, :, :].bitcast(F32).rearrange("p j (b q) -> p j b q", b=BPT),
                                    ALU.subtract).then_inc(A["olo"], 1)
                t = i - 2
                if live(t):
                    e.tensor_tensor(k_lo[:, :], kT[:, :, :].rearrange("p c t -> p (c t)"), k_hi[:, :],
                                    ALU.subtract).then_inc(A["klo"], 1)
                if live(i):
                    t = i
                    upto(e, "pk", t)
                    upto(e, "tk", t - 2)
                    clip(t, B3, kn[t % 2][:, :], "ck")
                    upto(e, "ck", t)
                    e.bn_stats(stats[t % 2][:, 1, :], kn[t % 2][:, :]).then_inc(A["bn"], 1)
                    upto(e, "bn", t)
                    for n in range(2):
                        m = e.bn_aggr(mean_var[t % 2][:, n, :], stats[t % 2][:, n, :])
                    m.then_inc(A["aggr"], 1)
                    upto(e, "aggr", t)
                    e.tensor_scalar(var_eps[t % 2][:, :], mean_var[t % 2][:, :, 1], EPS, None, ALU.add) \
                        .then_inc(A["eps"], 1)
                    upto(e, "pv", t)
                    upto(e, "vlo", t - 2)
                    clip(t, B5, vf[t % 2][:, :], "cv")
                t = i - 2
                if live(t):
                    upto(e, "klo", t)
                    e.tensor_tensor(kx_lo[:, :, :, :], wide(k_lo), mask, ALU.mult).then_inc(A["kxlo"], 1)
                    upto(e, "qhi", t)
                    e.tensor_tensor(q_lo[:, :, :], qT[:, :, :], q_hi[:, :, :], ALU.subtract) \
                        .then_inc(A["qlo"], 1)
                if live(i):
                    t = i
                    upto(e, "rstd", t)
                    upto(e, "kn", t - 2)
                    e.scalar_tensor_tensor(shift[t % 2][:, :], mean_var[t % 2][:, :, 0], -1.0,
                                           rstd[t % 2][:, :], ALU.mult, ALU.mult).then_inc(A["shift"], 1)
                t = i - 3
                if live(t):
                    upto(e, "vlo", t)
                    upto(e, "vhi", t)
                    upto(e, "o", t - 1)
                    dims = [P, HEADS, BPT, HD]
                    own = vmask[:, 0:BPT * HD].rearrange("p (o b d) -> p o b d", o=1, b=BPT).broadcast_to(dims)
                    for vx, v, name in ((vx_hi, v_hi[t % VR], "vxhi"), (vx_lo, v_lo[t % VR], "vxlo")):
                        e.tensor_tensor(vx[:, :, 0:BPT * HD].rearrange("p h (b d) -> p h b d", b=BPT),
                                        v[:, :, :].rearrange("p h (o d) -> p h o d", o=1).broadcast_to(dims),
                                        own, ALU.mult).then_inc(A[name], 1)
                t = i - 4
                if live(t):
                    upto(e, "r", t)
                    if t >= 2:
                        e.wait_ge(a_store[t % 2], 16 * (t // 2))
                    e.tensor_tensor(x1t[t % 2][:, :], B6, xt[t % XR][:, :], ALU.add).then_inc(A["x1"], 1)
                for n in made_in(i):
                    low(n)

        @block.gpsimd
        def _(e):
            def style(t):
                upto(e, "h", t - 2)
                e.wait_ge(a_x[t % XR], 32 * (t // XR + 1))
                e.tensor_tensor(style_bd[t % 2][:, :, :],
                                style_rows[t % XR][:, :].rearrange("p (o d) -> p o d", o=1)
                                .broadcast_to([P, BPT, SEQ]),
                                cst[:, C_WMASK:C_ROW].rearrange("p (j d) -> p j d", j=BPT), ALU.mult) \
                    .then_inc(A["style"], 1)

            def rows(idx, i):
                return bass.IndirectOffsetOnAxis(ap=idx[:, i:i + 1], axis=0)

            def gather(t):
                upto(e, "x1", t - XR)
                e.indirect_dma_start(out=xt[t % XR][:, :], out_offset=None, in_=x, in_offset=rows(tile_rows, t)) \
                    .then_inc(a_x[t % XR], 16)
                e.indirect_dma_start(out=style_rows[t % XR][:, :], out_offset=None, in_=style_w,
                                     in_offset=rows(style_idx, t)).then_inc(a_x[t % XR], 16)

            def gather_slot(s):
                last = min(s, T - 1)
                for n in (last, last - 1):
                    if n >= 0:
                        e.wait_ge(a_store[n % 2], 16 * (n // 2 + 1))
                if s >= 2:
                    e.wait_ge(d_t, s - 1)
                there = P * (last + 1)
                e.indirect_dma_start(out=xg[s % 2][:, :], out_offset=None, in_=x1_rows[0:there, :],
                                     in_offset=rows(slot_rows, s), bounds_check=there - 1,
                                     oob_is_err=False).then_inc(d_x[s % 2], 16)

            def scatter_slot(s):
                e.wait_ge(d_mc, s + 1)
                e.indirect_dma_start(out=y_rows, out_offset=rows(slot_rows, s), in_=ys[s % 2][:, :],
                                     in_offset=None, bounds_check=TOKENS - 1,
                                     oob_is_err=False).then_inc(d_y[s % 2], 16)

            for n in range(2):
                e.memset(xg[n][:, :], 0.0).then_inc(d_zero, 1)
            e.wait_ge(d_zero, 2)
            e.wait_ge(s_tables, 1)
            for t in range(3):
                gather(t)
            e.wait_ge(s_tables, 2)
            style(0)
            style(1)
            for i in range(STEPS + 1):
                live = lambda t: 0 <= t < T
                t = i - 3
                if live(t):
                    upto(e, "max", t)
                    e.tensor_tensor(probs[:, :, :], probs[:, :, :],
                                    row_max[:, :].rearrange("p (h o) -> p h o", o=1)
                                    .broadcast_to([P, HEADS, SEQ]), ALU.subtract).then_inc(A["sub"], 1)
                if 0 <= i - LAG - 1 < SLOTS:
                    scatter_slot(i - LAG - 1)
                if 0 <= i - LAG + 1 < SLOTS:
                    gather_slot(i - LAG + 1)
                if live(i + 2):
                    style(i + 2)
                if live(i + 3):
                    gather(i + 3)
                if live(t):
                    upto(e, "phi", t)
                    upto(e, "o", t - 1)
                    e.tensor_tensor(p_lo[:, :], probsT[:, :], p_hi[:, :], ALU.subtract).then_inc(A["plo"], 1)
                if live(i):
                    t = i
                    upto(e, "eps", t)
                    e.tensor_tensor(rstd[t % 2][:, :], var_eps[t % 2][:, :], cst[:, C_POW:C_POW + 2], ALU.pow) \
                        .then_inc(A["rstd"], 1)
                    upto(e, "vhi", t)
                    upto(e, "vxlo", t - VR)
                    e.tensor_tensor(v_lo[t % VR][:, :, :], vf[t % 2][:, :].rearrange("p (h d) -> p h d", h=HEADS),
                                    v_hi[t % VR][:, :, :], ALU.subtract).then_inc(A["vlo"], 1)
            for n in range(2):
                e.wait_ge(d_y[n], 16 * (SLOTS // 2))

    TOK = GROUP * P
    yt = w2t
    total = ys
    ot = [xg[0], xg[1], xgT]
    x1g = [sb(f"x1g{i}", [P, DM]) for i in range(GROUP)]
    yT_hi = [sb(f"yT_hi{i}", [P, KC, TOK], F32R) for i in range(2)]
    yT_lo = [sb(f"yT_lo{i}", [P, KC, TOK], F32R) for i in range(2)]
    gates = sb("gates", [2 * EXPERTS, TOK])
    gates_t = sb("gates_t", [P, GROUP, 2 * EXPERTS])
    logits = sb("logits", [P, GROUP, EXPERTS])
    best = sb("best", [P, GROUP, 8])
    weight = [sb(f"weight{i}", [P, GROUP]) for i in range(2)]
    act = [sb(f"act{i}", [P, TOK]) for i in range(3)]
    u_hi = sb("u_hi", [P, FC, TOK], F32R)
    u_lo = sb("u_lo", [P, FC, TOK], F32R)
    lnw = sb("lnw", [P, 2, DM])
    fstats = sb("fstats", [P, 6])
    fmv = [sb(f"fmv{i}", [P, 2]) for i in range(2)]
    fve = [sb(f"fve{i}", [P, 1]) for i in range(2)]
    frstd = [sb(f"frstd{i}", [P, 1]) for i in range(2)]
    fshift = [sb(f"fshift{i}", [P, 1]) for i in range(2)]

    f_ln = sem("f_ln")
    f_y, f_x1 = [sem(f"f_y{i}") for i in range(2)], [sem(f"f_res{i}") for i in range(GROUP)]
    f_out = [sem(f"f_out{i}") for i in range(3)]
    fn = ("t", "hi", "lo", "g", "gc", "gt", "gtc", "log", "best", "w", "u", "relu", "act", "uhi", "ulo", "dr", "route", "tot",
          "bn", "aggr", "eps", "rstd", "shift", "norm", "gam", "bet", "res")
    S = {n: sem(f"f_{n}_") for n in fn}

    with nc.Block() as block:
        @block.sync
        def _(e):
            e.dma_start(lnw[:, :, :].rearrange("p a n -> p (a n)"), ffn_ln.broadcast_to([P, 2 * DM])) \
                .then_inc(f_ln, 16)

            def load(m):
                rows = slice(TOK * m, TOK * m + TOK)
                if m >= 2:
                    e.wait_ge(S["t"], KC * (m - 1))
                e.dma_start(yt[m % 2][:, :, :], y_rows[rows, :].rearrange("(t p) n -> p t n", p=P)) \
                    .then_inc(f_y[m % 2], 16)

            def load_x1(n):
                if n >= GROUP:
                    e.wait_ge(S["res"], n - GROUP + 1)
                e.dma_start(x1g[n % GROUP][:, :], x1_rows[P * n:P * n + P, :]).then_inc(f_x1[n % GROUP], 16)

            load(0)
            load(1)
            for n in range(GROUP):
                load_x1(n)
            for m in range(GROUPS):
                for t in range(GROUP):
                    n = GROUP * m + t
                    if n + GROUP < TILES:
                        load_x1(n + GROUP)
                if m + 2 < GROUPS:
                    load(m + 2)

        @block.tensor
        def _(e):
            def turn(m):
                e.wait_ge(f_y[m % 2], 16 * (m // 2 + 1))
                for c in range(KC):
                    n = KC * m + c
                    if n >= 2:
                        e.wait_ge(S["lo"], n - 1)
                    if c < 2 and m:
                        e.wait_ge(S["gtc"], m)
                        e.wait_ge(S["gc"], m)
                    for t in range(GROUP):
                        k = e.transpose((B4, B5)[c % 2][:, P * t:P * t + P],
                                        yt[m % 2][:, t, P * c:P * c + P], ident)
                    k.then_inc(S["t"], 1)

            def gate_products(m):
                e.wait_ge(S["lo"], KC * (m + 1))
                for c in range(KC):
                    w = gate_hl[:, c, :, :].rearrange("p a n -> p (a n)")
                    for n, y in enumerate((yT_hi, yT_lo)):
                        k = e.matmul(B4[0:2 * EXPERTS, :], w, y[m % 2][:, c, :],
                                     start=(c == 0 and n == 0), stop=(c == KC - 1 and n == 1))
                k.then_inc(S["g"], 1)

            def turn_gates(m):
                e.wait_ge(S["gc"], m + 1)
                for t in range(GROUP):
                    k = e.transpose(B5[:, 2 * EXPERTS * t:2 * EXPERTS * (t + 1)],
                                    gates[:, P * t:P * t + P], cst[0:2 * EXPERTS, C_IDENT:C_IDENT + 2 * EXPERTS])
                k.then_inc(S["gt"], 1)

            def up(m):
                e.wait_ge(S["lo"], KC * (m + 1))
                for f in range(FC):
                    n = FC * m + f
                    if n >= 2:
                        e.wait_ge(S["relu"], n - 1)
                    cols = slice(P * f, P * f + P)
                    for c in range(KC):
                        for k, (a, b) in enumerate(((up_hi, yT_hi), (up_hi, yT_lo), (up_lo, yT_hi))):
                            i = e.matmul((B2, B3)[n % 2], a[:, c, cols], b[m % 2][:, c, :],
                                         start=(c == 0 and k == 0), stop=(c == KC - 1 and k == 2))
                    i.then_inc(S["u"], 1)

            def down(m):
                for t in range(GROUP):
                    n = GROUP * m + t
                    toks = slice(P * t, P * t + P)
                    if n >= 2:
                        e.wait_ge(S["tot"], n - 1)
                    into = pair[:, n % 2, :]
                    route = (B6, B7)[n % 2]
                    for c in range(KC):
                        for k, (a, b) in enumerate(((yT_hi, route_hi), (yT_hi, route_lo), (yT_lo, route_hi))):
                            e.matmul(route, a[m % 2][:, c, toks], b[:, c, :],
                                     start=(c == 0 and k == 0), stop=(c == KC - 1 and k == 2))
                    for f in range(FC):
                        if t == 0:
                            e.wait_ge(S["ulo"], FC * m + f + 1)
                        for k, (a, b) in enumerate(((u_hi, down_hi), (u_hi, down_lo), (u_lo, down_hi))):
                            i = e.matmul(into, a[:, f, toks], b[:, f, :],
                                         start=(f == 0 and k == 0), stop=(f == FC - 1 and k == 2))
                    i.then_inc(S["dr"], 1)

            turn(0)
            gate_products(0)
            for m in range(GROUPS):
                up(m)
                turn_gates(m)
                if m + 1 < GROUPS:
                    turn(m + 1)
                    gate_products(m + 1)
                down(m)

        @block.scalar
        def _(e):
            def high(m):
                for c in range(KC):
                    n = KC * m + c
                    e.wait_ge(S["t"], n + 1)
                    if m >= 2 and c == 0:
                        e.wait_ge(S["dr"], GROUP * (m - 1))
                    e.activation(yT_hi[m % 2][:, c, :], (B4, B5)[c % 2], ACT.Copy).then_inc(S["hi"], 1)
                e.wait_ge(S["g"], m + 1)
                if m:
                    e.wait_ge(S["gt"], m)
                e.activation(gates[:, :], B4[0:2 * EXPERTS, :], ACT.Copy).then_inc(S["gc"], 1)

            high(0)
            for m in range(GROUPS):
                for f in range(FC + 1):
                    n = FC * m + f
                    if f < FC:
                        e.wait_ge(S["u"], n + 1)
                        if n >= 3:
                            e.wait_ge(S["ulo"], n - 2)
                        e.activation(act[n % 3][:, :], (B2, B3)[n % 2], ACT.Relu).then_inc(S["relu"], 1)
                    if f:
                        e.wait_ge(S["act"], n)
                        if m and f == 1:
                            e.wait_ge(S["dr"], GROUP * m)
                        e.activation(u_hi[:, f - 1, :], act[(n - 1) % 3][:, :], ACT.Copy).then_inc(S["uhi"], 1)
                if m + 1 < GROUPS:
                    high(m + 1)
                for t in range(GROUP):
                    n = GROUP * m + t
                    e.wait_ge(S["dr"], n + 1)
                    e.wait_ge(S["w"], m + 1)
                    if n >= 2:
                        e.wait_ge(S["gam"], n - 1)
                    e.activation(total[n % 2][:, :], (B6, B7)[n % 2], ACT.Identity,
                                 scale=weight[m % 2][:, t:t + 1]).then_inc(S["route"], 1)
                    e.wait_ge(S["shift"], n + 1)
                    e.activation(total[n % 2][:, :], total[n % 2][:, :], ACT.Identity,
                                 bias=fshift[n % 2][:, 0:1], scale=frstd[n % 2][:, 0:1]) \
                        .then_inc(S["norm"], 1)

        @block.vector
        def _(e):
            def low(m):
                for c in range(KC):
                    n = KC * m + c
                    e.wait_ge(S["hi"], n + 1)
                    e.tensor_tensor(yT_lo[m % 2][:, c, :], (B4, B5)[c % 2], yT_hi[m % 2][:, c, :].bitcast(F32),
                                    ALU.subtract).then_inc(S["lo"], 1)

            low(0)
            for m in range(GROUPS):
                for f in range(FC):
                    n = FC * m + f
                    e.wait_ge(S["relu"], n + 1)
                    e.tensor_tensor(act[n % 3][:, :], act[n % 3][:, :], act[n % 3][:, :], ALU.mult) \
                        .then_inc(S["act"], 1)
                e.wait_ge(S["gt"], m + 1)
                e.tensor_copy(gates_t[:, :, :], B5[:, 0:GROUP * 2 * EXPERTS]
                              .rearrange("p (t n) -> p t n", t=GROUP)).then_inc(S["gtc"], 1)
                e.wait_ge(S["gtc"], m + 1)
                e.tensor_tensor(logits[:, :, :], gates_t[:, :, 0:EXPERTS], gates_t[:, :, EXPERTS:2 * EXPERTS],
                                ALU.add).then_inc(S["log"], 1)
                e.wait_ge(S["log"], m + 1)
                for t in range(GROUP):
                    k = e.max(best[:, t, :], logits[:, t, :])
                k.then_inc(S["best"], 1)
                e.wait_ge(S["best"], m + 1)
                e.tensor_tensor(weight[m % 2][:, :], best[:, :, 0], best[:, :, 1], ALU.add).then_inc(S["w"], 1)
                e.wait_ge(S["w"], m + 1)
                if m + 1 < GROUPS:
                    low(m + 1)
                for t in range(GROUP):
                    n = GROUP * m + t
                    b = n % 2
                    e.wait_ge(S["route"], n + 1)
                    e.tensor_tensor(total[b][:, :], total[b][:, :], pair[:, b, :], ALU.add) \
                        .then_inc(S["tot"], 1)
                    e.wait_ge(S["tot"], n + 1)
                    e.bn_stats(fstats[:, :], total[b][:, :]).then_inc(S["bn"], 1)
                    e.wait_ge(S["bn"], n + 1)
                    e.bn_aggr(fmv[b][:, :], fstats[:, :]).then_inc(S["aggr"], 1)
                    e.wait_ge(S["aggr"], n + 1)
                    e.tensor_scalar(fve[b][:, :], fmv[b][:, 1:2], EPS, None, ALU.add).then_inc(S["eps"], 1)
                    e.wait_ge(S["rstd"], n + 1)
                    e.scalar_tensor_tensor(fshift[b][:, :], fmv[b][:, 0:1], -1.0, frstd[b][:, :],
                                           ALU.mult, ALU.mult).then_inc(S["shift"], 1)
                    e.wait_ge(S["norm"], n + 1)
                    if n == 0:
                        e.wait_ge(f_ln, 16)
                    if n >= 3:
                        e.wait_ge(f_out[n % 3], 16 * (n // 3))
                    e.tensor_tensor(ot[n % 3][:, :], total[b][:, :], lnw[:, 0, :], ALU.mult) \
                        .then_inc(S["gam"], 1)
                    e.wait_ge(S["gam"], n + 1)
                    e.tensor_tensor(ot[n % 3][:, :], ot[n % 3][:, :], lnw[:, 1, :], ALU.add) \
                        .then_inc(S["bet"], 1)
                    e.wait_ge(S["bet"], n + 1)
                    e.wait_ge(f_x1[t], 16 * (m + 1))
                    e.tensor_tensor(ot[n % 3][:, :], ot[n % 3][:, :], x1g[t][:, :], ALU.add) \
                        .then_inc(S["res"], 1)

        @block.gpsimd
        def _(e):
            def store(n):
                e.wait_ge(S["res"], n + 1)
                e.indirect_dma_start(out=out, out_offset=bass.IndirectOffsetOnAxis(
                    ap=tile_rows[:, n:n + 1], axis=0), in_=ot[n % 3][:, :], in_offset=None) \
                    .then_inc(f_out[n % 3], 16)

            for m in range(GROUPS):
                for f in range(FC):
                    n = FC * m + f
                    e.wait_ge(S["uhi"], n + 1)
                    if m and f == 0:
                        e.wait_ge(S["dr"], GROUP * m)
                    e.tensor_tensor(u_lo[:, f, :], act[n % 3][:, :], u_hi[:, f, :].bitcast(F32), ALU.subtract) \
                        .then_inc(S["ulo"], 1)
                for t in range(GROUP):
                    n = GROUP * m + t
                    e.wait_ge(S["eps"], n + 1)
                    e.tensor_tensor(frstd[n % 2][:, :], fve[n % 2][:, :], cst[:, C_POW:C_POW + 1], ALU.pow) \
                        .then_inc(S["rstd"], 1)
                    if n:
                        store(n - 1)
            store(TILES - 1)
            for n in range(3):
                e.wait_ge(f_out[n], 16 * ((TILES - n + 2) // 3))
    top.close()


def chunked(w):
    return np.ascontiguousarray(w.reshape(-1, P, w.shape[1]).transpose(1, 0, 2))


def kernel(x, itok_B_0_15, itok_B_3_7, L0_cond_weights, L0_attn_w_qkv, L0_attn_q_ln_w, L0_attn_q_ln_b,
           L0_attn_k_ln_w, L0_attn_k_ln_b, L0_attn_w_out, L0_cond2_weight, L0_ffn_gate_w, L0_ffn_up_w,
           L0_ffn_down_w, L0_ffn_fc1_w, L0_ffn_fc2_w, L0_ffn_expert_w, L0_ffn_ln_gamma, L0_ffn_ln_beta):
    import concourse.bacc as bacc
    from concourse.bass_utils import run_bass_kernel_spmd

    a = lambda v: np.asarray(v)
    side = lambda v: a(v).reshape(KC, P).T
    arrays = {
        "x": a(x).reshape(TOKENS, DM),
        "style_ids": a(itok_B_0_15).reshape(1, BATCHES),
        "adapter_ids": a(itok_B_3_7).reshape(1, BATCHES),
        "style_w": a(L0_cond_weights).reshape(STYLES * SEQ, SEQ),
        "wqkv": a(L0_attn_w_qkv).reshape(3, DM, KC, P).transpose(3, 0, 2, 1),
        "wo": a(L0_attn_w_out).reshape(DM, HG, BPT, HD).transpose(1, 3, 2, 0).reshape(P, BPT, DM),
        "qk_ln": np.concatenate([side(v) for v in (L0_attn_q_ln_w, L0_attn_q_ln_b, L0_attn_k_ln_w,
                                                   L0_attn_k_ln_b)], axis=1),
        "w2": a(L0_cond2_weight).reshape(ADAPTERS, DM, KC, P).transpose(3, 0, 2, 1)
        .reshape(P, ADAPTERS, KC * DM),
        "w_up": chunked(a(L0_ffn_up_w)),
        "w_down": chunked(a(L0_ffn_down_w)),
        "fc1t": chunked(a(L0_ffn_fc1_w).T),
        "expert": chunked(a(L0_ffn_expert_w)),
        "fc2": chunked(a(L0_ffn_fc2_w)),
        "gate": chunked(a(L0_ffn_gate_w)),
        "ffn_ln": np.concatenate([a(L0_ffn_ln_gamma), a(L0_ffn_ln_beta)]).reshape(1, 2 * DM),
        "consts": constants(),
    }
    arrays = {n: np.ascontiguousarray(v) for n, v in arrays.items()}
    nc = bacc.Bacc("TRN2", target_bir_lowering=False, num_devices=1)
    aps = {n: nc.dram_tensor(f"in_{n}", v.shape, mybir.dt.from_np(v.dtype), kind="ExternalInput").ap()
           for n, v in arrays.items()}
    aps["out"] = nc.dram_tensor("out", (TOKENS, DM), F32, kind="ExternalOutput").ap()
    program(nc, **aps)
    r = run_bass_kernel_spmd(nc, [{f"in_{n}": v for n, v in arrays.items()}], core_ids=[0])
    return r.results[0]["out"].reshape(BATCHES, SEQ, DM)
```

```python
from contextlib import ExitStack

import numpy as np

import concourse.bass as bass
from concourse import mybir

F32 = mybir.dt.float32
F32R = mybir.dt.float32r
BF16 = mybir.dt.bfloat16
I32 = mybir.dt.int32
ALU = mybir.AluOpType
ACT = mybir.ActivationFunctionType
AX = mybir.AxisListType

P = 128
BATCHES, SEQ, DM = 128, 32, 512
TOKENS = BATCHES * SEQ
BPT = P // SEQ
TILES = TOKENS // P
KC = DM // P
HEADS, HD = 32, 16
HPC = P // HD
HG = HEADS // BPT
STYLES = 16
ADAPTERS = 8
SLOTS = (BATCHES + ADAPTERS * (BPT - 1)) // BPT
INNER = 1024
FC = INNER // P
LAT = 256
LC = LAT // P
EXPERTS = 8
GROUP = 4
GROUPS = TILES // GROUP
CLIP = 8.0
SCALE = HD ** -0.5
EPS = 1e-5
MASKED = -1e30
ABSENT = 2.0 ** 17

C_BIAS = 0
C_IDENT = C_BIAS + HEADS * SEQ
C_KMASK = C_IDENT + P
C_VMASK = C_KMASK + HPC * SEQ
VW = BPT * HD + BPT
C_WMASK = C_VMASK + VW
C_ROW = C_WMASK + P
C_SLOT = C_ROW + P
C_VAL = C_SLOT + SLOTS * BPT
C_COL = C_VAL + SEQ
C_PMOD = C_COL + 1
C_POW = C_PMOD + 1
C_SIZE = C_POW + 2


def constants():
    p = np.arange(P)
    q = p % SEQ
    c = np.zeros((P, C_SIZE), np.float32)
    m = np.arange(1, HEADS + 1, dtype=np.float32) * np.float32(8 / HEADS)
    slopes = (np.float32(1.0) / np.power(np.float32(2.0), m)).astype(np.float32)
    rel = (np.arange(SEQ)[None, :] - q[:, None]).astype(np.float32)
    bias = slopes[None, :, None] * rel[:, None, :]
    c[:, C_BIAS:C_IDENT] = np.where(rel[:, None, :] <= 0, bias, np.float32(MASKED)).reshape(P, -1)
    c[:, C_IDENT:C_KMASK] = np.eye(P)
    c[:, C_KMASK:C_VMASK] = np.repeat(p[:, None] // HD == np.arange(HPC)[None, :], SEQ, axis=1)
    own = p[:, None] // SEQ == np.arange(BPT)[None, :]
    c[:, C_VMASK:C_VMASK + BPT * HD] = np.repeat(own, HD, axis=1)
    c[:, C_VMASK + BPT * HD:C_WMASK] = own
    c[:, C_WMASK:C_ROW] = np.repeat(own, SEQ, axis=1)
    c[:, C_ROW:C_SLOT] = p[None, :]
    c[:, C_SLOT:C_VAL] = np.arange(SLOTS * BPT)[None, :]
    c[:, C_VAL:C_COL] = (SEQ * p - ABSENT)[:, None]
    c[:, C_COL] = p
    c[:, C_PMOD] = q
    c[:, C_POW:C_POW + 2] = -0.5
    return c


def program(nc, x, style_ids, adapter_ids, style_w, wqkv, wo, qk_ln, w2, w_up, w_down, fc1t, expert,
            fc2, gate, ffn_ln, consts, out):
    x1_rows = nc.dram_tensor("x1_rows", [TOKENS, DM], F32, kind="Internal").ap()
    y_rows = nc.dram_tensor("y_rows", [TOKENS, DM], F32, kind="Internal").ap()
    top = ExitStack()

    def tiles_in(stack):
        def sb(name, shape, dt=F32):
            return stack.enter_context(nc.sbuf_tensor(name, shape, dt))
        return sb

    sb = tiles_in(top)

    def psum(name, shape, dt=F32):
        return top.enter_context(nc.psum_tensor(name, shape, dt))

    def sem(name):
        return top.enter_context(nc.semaphore(name))

    cst = sb("cst", [P, C_SIZE])
    ident = cst[:, C_IDENT:C_KMASK]
    bias = cst[:, C_BIAS:C_IDENT].rearrange("p (h k) -> p h k", h=HEADS)
    kmask = sb("kmask", [P, HPC * SEQ], BF16)
    vmask = sb("vmask", [P, VW], BF16)
    qkln = sb("qkln", [P, 4 * KC])
    slot_rows = sb("slot_rows", [P, SLOTS], I32)
    slot_adapter = sb("slot_adapter", [1, SLOTS], I32)
    bank = [psum(f"bank{i}", [P, DM]) for i in range(2, 8)]
    pair = psum("pair", [P, 2, DM])
    B2, B3, B4, B5, B6, B7 = (b[:, :] for b in bank)

    tile_rows = sb("tile_rows", [P, TILES], I32)
    style_idx = sb("style_idx", [P, TILES], I32)
    split = ExitStack()
    ssb = tiles_in(split)
    w2_lo = ssb("w2_lo", [P, KC, DM], F32R)
    w2_hi = ssb("w2_hi", [P, KC, DM], F32R)
    xgT_hi = ssb("xgT_hi", [P, DM], F32R)
    xgT_lo = ssb("xgT_lo", [P, DM], F32R)
    split.close()
    w2t = [sb(f"w2t{i}", [P, KC, DM]) for i in range(2)]
    xgT = [sb(f"xgT{i}", [P, DM]) for i in range(2)]
    xg = [sb(f"xg{i}", [P, DM]) for i in range(2)]
    ys = [sb(f"ys{i}", [P, DM]) for i in range(2)]

    weights = ExitStack()
    wsb = tiles_in(weights)
    wqkv_hi = wsb("wqkv_hi", [P, 3, KC, DM], F32R)
    wqkv_lo = wsb("wqkv_lo", [P, 3, KC, DM], F32R)
    wo_hi = wsb("wo_hi", [P, BPT, DM], F32R)
    wo_lo = wsb("wo_lo", [P, BPT, DM], F32R)

    XR, VR = 8, 5
    att = ExitStack()
    asb = tiles_in(att)
    xt = [asb(f"xt{i}", [P, DM]) for i in range(XR)]
    style_rows = [asb(f"style_rows{i}", [P, SEQ]) for i in range(XR)]
    style_bd = [asb(f"style_bd{i}", [P, BPT, SEQ]) for i in range(2)]
    h_hi = [asb(f"h_hi{i}", [P, KC, P], F32R) for i in range(2)]
    h_lo = [asb(f"h_lo{i}", [P, KC, P], F32R) for i in range(2)]
    qn = [asb(f"qn{i}", [P, DM]) for i in range(2)]
    kn = [asb(f"kn{i}", [P, DM]) for i in range(2)]
    stats = [asb(f"stats{i}", [P, 2, 6]) for i in range(2)]
    mean_var = [asb(f"mean_var{i}", [P, 2, 2]) for i in range(2)]
    var_eps = [asb(f"var_eps{i}", [P, 2]) for i in range(2)]
    rstd = [asb(f"rstd{i}", [P, 2]) for i in range(2)]
    shift = [asb(f"shift{i}", [P, 2]) for i in range(2)]
    qT = asb("qT", [P, KC, P])
    kT = asb("kT", [P, KC, P])
    q_hi = asb("q_hi", [P, KC, P], BF16)
    k_hi = asb("k_hi", [P, KC * P], BF16)
    v_hi = [asb(f"v_hi{i}", [P, HEADS, HD], BF16) for i in range(VR)]
    v_lo = [asb(f"v_lo{i}", [P, HEADS, HD], BF16) for i in range(VR)]
    p_hi = asb("p_hi", [P, HEADS * SEQ], BF16)
    p_lo = asb("p_lo", [P, HEADS * SEQ], BF16)
    o_hi = asb("o_hi", [P, BPT, P], F32R)
    o_lo = asb("o_lo", [P, BPT, P], F32R)
    x1t = [asb(f"x1t{i}", [P, DM]) for i in range(2)]

    prep = ExitStack()
    psb = tiles_in(prep)
    stage = [psb(f"stage{i}", [P, KC, DM]) for i in range(4)]
    ids_row = psb("ids_row", [P, BATCHES], I32)
    ids_col = psb("ids_col", [P, 1], I32)
    style_col = psb("style_col", [P, 1], I32)
    idr = psb("idr", [P, BATCHES])
    idc = psb("idc", [P, 1])
    stylec = psb("stylec", [P, 1])
    keyr = psb("keyr", [P, BATCHES])
    keyc = psb("keyc", [P, 1])
    before = psb("before", [P, BATCHES])
    after = psb("after", [P, BATCHES])
    same = psb("same", [P, BATCHES])
    rank = psb("rank", [P, 1])
    sorted_row = psb("sorted_row", [P, 1])
    at_rank = psb("at_rank", [P, BATCHES])
    style_of = psb("style_of", [P, SEQ])
    row_of = psb("row_of", [P, SEQ])
    within = psb("within", [P, 1])
    within_i = psb("within_i", [P, 1], I32)
    place_i = psb("place_i", [P, 1], I32)
    place = psb("place", [P, 1])
    first = psb("first", [P, 1])
    slot_no = psb("slot_no", [P, 1])
    column = psb("column", [P, 1])
    onehot = psb("onehot", [P, SLOTS * BPT])
    table_f = [psb(f"table_f{i}", [P, SLOTS]) for i in range(4)]
    prep.close()

    vx_hi = asb("vx_hi", [P, HEADS, VW], BF16)
    vx_lo = asb("vx_lo", [P, HEADS, VW], BF16)
    on = asb("on", [P, BPT, HG, HD])
    row_max = asb("row_max", [P, HEADS])
    recip = asb("recip", [P, 2, 4, BPT])
    make = ExitStack()
    msb = tiles_in(make)
    probs = msb("probs", [P, HEADS, SEQ])
    probsT = msb("probsT", [P, HEADS * SEQ])
    vf = [msb(f"vf{i}", [P, DM]) for i in range(2)]
    k_lo = msb("k_lo", [P, KC * P], BF16)
    q_lo = msb("q_lo", [P, KC, P], BF16)
    kx_hi = msb("kx_hi", [P, KC * BPT, HPC, SEQ], BF16)
    kx_lo = msb("kx_lo", [P, KC * BPT, HPC, SEQ], BF16)
    make.close()
    fc1_sb = msb("fc1_sb", [P, LC, DM])
    fc2_sb = msb("fc2_sb", [P, LC, DM])
    latT = msb("latT", [P, LC, DM])
    ex_sb = msb("ex_sb", [P, LC, LAT])
    raw = [msb(f"raw{i}", [P, KC, DM]) for i in range(2)]
    gate_raw = msb("gate_raw", [P, KC, EXPERTS])
    make.close()

    s_cst, s_ids, s_masks = sem("s_cst"), sem("s_ids"), sem("s_masks")
    s_stage = [sem(f"s_stage{i}") for i in range(4)]
    s_whi, s_wlo = sem("s_whi"), sem("s_wlo")
    s_t = sem("s_t")
    s_tp = sem("s_tp")
    s_tables = sem("s_tables")
    STEP_AT_RANK, STEP_FIRST, STEP_ONEHOT = 9, 21, 24

    a_x = [sem(f"a_load{i}") for i in range(XR)]
    a_store = [sem(f"a_store{i}") for i in range(2)]
    names = ("style", "h", "hhi", "hlo", "pq", "pk", "pv", "cq", "ck", "bn", "aggr", "eps", "rstd", "shift",
             "qn", "kn", "tq", "tk", "qT", "kT", "qhi", "qlo", "khi", "klo", "kxhi", "kxlo", "cv", "vhi",
             "vlo", "vxhi", "vxlo", "vx1", "s", "sb", "max", "sub", "exp", "pT", "phi", "plo", "o", "rec",
             "on", "ot", "ohi", "olo", "r", "x1", "mask")
    A = {n: sem(f"a_{n}") for n in names}
    PER = {"bn": 2, "sb": 2, "on": 2}
    T = TILES
    LAG = 6
    STEPS = T + 4
    TAIL = STEPS - LAG
    SPLIT = T - LAG

    def upto(e, name, i):
        if i >= 0:
            e.wait_ge(A[name], PER.get(name, 1) * (i + 1))

    att.close()
    weights.close()

    TOK = GROUP * P
    up_hi = sb("up_hi", [P, KC, INNER], F32R)
    up_lo = sb("up_lo", [P, KC, INNER], F32R)
    route_hi = sb("route_hi", [P, KC, DM], F32R)
    route_lo = sb("route_lo", [P, KC, DM], F32R)
    down_hi = sb("down_hi", [P, FC, DM], F32R)
    down_lo = sb("down_lo", [P, FC, DM], F32R)
    gate_hl = sb("gate_hl", [P, KC, 2, EXPERTS], F32R)
    yt = [sb("yt0", [P, GROUP, DM]), w2t[0]]
    late = ExitStack()
    raw += [tiles_in(late)(f"raw{i}", [P, KC, DM]) for i in (2, 3)]
    late.close()
    yT_hi, yT_lo = [None, None], [None, None]
    for i in (1, 0):
        yT_hi[i] = sb(f"yT_hi{i}", [P, KC, TOK], F32R)
        yT_lo[i] = sb(f"yT_lo{i}", [P, KC, TOK], F32R)
    x1g = [w2t[1][:, i, :] for i in range(GROUP)]
    lnw = sb("lnw", [P, 2, DM])
    act = [sb(f"act{i}", [P, TOK]) for i in range(3)]
    gates = sb("gates", [2 * EXPERTS, TOK])
    gates_t = sb("gates_t", [P, GROUP, 2 * EXPERTS])
    logits = sb("logits", [P, GROUP, EXPERTS])
    best = sb("best", [P, GROUP, 8])
    weight = [sb(f"weight{i}", [P, GROUP]) for i in range(2)]
    fstats = sb("fstats", [P, 6])
    fmv = [sb(f"fmv{i}", [P, 2]) for i in range(2)]
    fve = [sb(f"fve{i}", [P, 1]) for i in range(2)]
    frstd = [sb(f"frstd{i}", [P, 1]) for i in range(2)]
    u_hi = sb("u_hi", [P, FC, TOK], F32R)
    u_lo = sb("u_lo", [P, FC, TOK], F32R)
    total = ys
    ot = [xg[0], xg[1], xgT[0]]

    m_raw, m_fc = [sem(f"m_raw{i}") for i in range(4)], sem("m_fc")
    m_hi, m_lo, m_lat, m_latc, m_route = sem("m_hi"), sem("m_lo"), sem("m_lat"), sem("m_latc"), sem("m_route")
    d_zero, d_w2, d_x = sem("d_zero"), [sem("d_w20"), sem("d_w21")], [sem("d_x0"), sem("d_x1")]
    d_y = [sem("d_y0"), sem("d_y1")]
    d_t, d_tc, d_tl, d_m, d_mc = sem("d_t"), sem("d_tc"), sem("d_tl"), sem("d_m"), sem("d_mc")
    d_whi, d_wlo = sem("d_whi"), sem("d_wlo")
    f_ln = sem("f_ln")
    f_y, f_x1 = [sem(f"f_y{i}") for i in range(2)], [sem(f"f_res{i}") for i in range(GROUP)]
    f_out = [sem(f"f_out{i}") for i in range(3)]
    fn = ("t", "hi", "lo", "g", "gc", "gt", "gtc", "log", "best", "w", "u", "relu", "act", "uhi", "ulo",
          "rp", "dr", "route", "tot", "bn", "aggr", "eps", "rstd", "gam", "bet", "res")
    S = {n: sem(f"f_{n}_") for n in fn}

    parts = {}

    def add_raw(name, w, hi, lo, cols, chunks, n):
        parts[name] = ((m_raw[n], 16), raw[n][:, :, :], hi[:, chunks, cols], lo[:, chunks, cols])
        return w[:, chunks, cols]

    def add_route(c):
        parts[f"route{c}"] = ((m_route, c + 1), (B2, B3)[c % 2], route_hi[:, c, :], route_lo[:, c, :])

    every, half = slice(0, KC), (slice(0, DM), slice(DM, 2 * DM))
    parts["gate"] = ((m_fc, 64), gate_raw[:, :, :], gate_hl[:, :, 0, :], gate_hl[:, :, 1, :])
    add_route(0)
    add_route(1)
    raw_from = [add_raw(f"up{n}", w_up, up_hi, up_lo, half[n], every, n) for n in range(2)]
    add_route(2)
    add_route(3)
    raw_from.append(add_raw("down0", w_down, down_hi, down_lo, half[0], slice(0, KC), 2))
    raw_from.append(add_raw("down1", w_down, down_hi, down_lo, half[0], slice(KC, FC), 3))
    order = list(parts)

    def made(name):
        return order.index(name) + 1

    ALL_MADE = len(order)

    def slot_banks(s):
        if s < SPLIT:
            return B7, B4
        if s < TAIL:
            return B7, B2
        return (B7, B6)[s % 2], pair[:, s % 2, :]

    def upto_product(e, s):
        before = s if s <= SPLIT else max(s - 1, SPLIT)
        if before:
            e.wait_ge(d_m, before)

    def last_slot(m):
        return min((BPT * GROUP * (m + 1) - 1 + (ADAPTERS - 1) * (BPT - 1)) // BPT, SLOTS - 1)

    with nc.Block() as block:
        @block.sync
        def _(e):
            e.dma_start(cst[:, C_WMASK:C_SIZE], consts[:, C_WMASK:C_SIZE]).then_inc(s_cst, 16)
            for dst, src in ((ids_row[:, :], adapter_ids.broadcast_to([P, BATCHES])),
                             (ids_col[:, :], adapter_ids.rearrange("o b -> b o")),
                             (style_col[:, :], style_ids.rearrange("o b -> b o")),
                             (qkln[:, :], qk_ln)):
                e.dma_start(dst, src).then_inc(s_ids, 16)
            def load_stage(n):
                e.dma_start(stage[n][:, :, :], wqkv[:, n] if n < 3 else wo).then_inc(s_stage[n], 16)

            load_stage(0)
            load_stage(1)
            e.wait_ge(a_x[0], 32)
            load_stage(2)
            e.dma_start(cst[:, 0:C_WMASK], consts[:, 0:C_WMASK]).then_inc(s_masks, 16)
            load_stage(3)
            e.wait_ge(s_tables, 2)

            def load_w2(s):
                upto_product(e, s)
                tile = w2t[0 if s < SPLIT else s % 2]
                adapter = e.value_load(slot_adapter[0:1, s:s + 1], min_val=0, max_val=ADAPTERS - 1)
                e.dma_start(tile[:, :, :].rearrange("p (o c) n -> p o (c n)", o=1),
                            w2[:, bass.ds(adapter, 1), :]).then_inc(d_w2[s % 2], 16)

            def load_raw(n):
                e.dma_start(raw[n][:, :, :], raw_from[n]).then_inc(m_raw[n], 16)

            def load_y(m):
                rows = slice(TOK * m, TOK * m + TOK)
                if m >= 2:
                    e.wait_ge(S["t"], KC * (m - 1))
                for s in (last_slot(m) - 1, last_slot(m)):
                    e.wait_ge(d_y[s % 2], 16 * (s // 2 + 1))
                e.dma_start(yt[m % 2][:, :, :], y_rows[rows, :].rearrange("(t p) n -> p t n", p=P)) \
                    .then_inc(f_y[m % 2], 16)

            def load_x1(n):
                if n >= GROUP:
                    e.wait_ge(S["res"], n - GROUP + 1)
                e.dma_start(x1g[n % GROUP], x1_rows[P * n:P * n + P, :]).then_inc(f_x1[n % GROUP], 16)

            for i in range(T + 5):
                t = i - 5
                if t >= 0:
                    upto(e, "x1", t)
                    e.dma_start(x1_rows[P * t:P * t + P, :], x1t[t % 2][:, :]).then_inc(a_store[t % 2], 16)
                s = i - LAG + 1
                if s >= 0:
                    load_w2(s)
                if i == T + 2:
                    upto(e, "s", T - 1)
                    load_raw(0)
                    load_raw(1)
                    upto(e, "plo", T - 1)
                    for dst, src in ((fc1_sb, fc1t), (ex_sb, expert), (fc2_sb, fc2), (gate_raw, gate)):
                        e.dma_start(dst[:, :, :], src).then_inc(m_fc, 16)
            for n in range(2):
                e.wait_ge(a_store[n], 16 * (T // 2))
            load_y(0)
            for s in range(T, SLOTS):
                load_w2(s)
                if s == T + 1:
                    load_raw(2)
            load_raw(3)
            e.dma_start(lnw[:, :, :].rearrange("p a n -> p (a n)"), ffn_ln.broadcast_to([P, 2 * DM])) \
                .then_inc(f_ln, 16)
            e.wait_ge(d_m, SLOTS)
            load_y(1)
            for n in range(GROUP):
                load_x1(n)
            for m in range(GROUPS):
                if m + 2 < GROUPS:
                    load_y(m + 2)
                for n in range(GROUP * (m + 1), min(GROUP * (m + 2), TILES)):
                    load_x1(n)

        @block.tensor
        def _(e):
            def style(t):
                e.wait_ge(a_x[t % XR], 32 * (t // XR + 1))
                upto(e, "style", t)
                if t > LAG + 1:
                    e.wait_ge(d_tl, t - LAG - 1)
                upto(e, "hlo", t - 1)
                for c in range(KC):
                    m = e.matmul(B7[:, P * c:P * c + P], xt[t % XR][:, P * c:P * c + P],
                                 style_bd[t % 2][:, :, :].rearrange("p j d -> p (j d)"), start=True, stop=True)
                m.then_inc(A["h"], 1)

            def project(t, n, into, name):
                upto(e, "hlo", t)
                e.wait_ge(s_wlo, n + 1)
                hi, lo = h_hi[t % 2], h_lo[t % 2]
                for c in range(KC):
                    for k, (a, b) in enumerate(((hi, wqkv_hi), (hi, wqkv_lo), (lo, wqkv_hi))):
                        m = e.matmul(into, a[:, c, :], b[:, n, c, :], start=(c == 0 and k == 0),
                                     stop=(c == KC - 1 and k == 2))
                m.then_inc(A[name], 1)

            def values(t):
                upto(e, "phi", t)
                upto(e, "plo", t)
                upto(e, "vxlo", t)
                e.wait_ge(A["vx1"], 1)
                upto(e, "sb", min(t + 1, T - 1))
                for g in range(HG):
                    dst = pair[:, g // 4, VW * (g % 4):VW * (g % 4) + VW]
                    for k, (a, b, w) in enumerate(((p_hi, vx_hi, VW), (p_lo, vx_hi, VW),
                                                   (p_hi, vx_lo, BPT * HD))):
                        for j in range(BPT):
                            h = BPT * g + j
                            m = e.matmul(dst[SEQ * j:SEQ * j + SEQ, 0:w], a[:, SEQ * h:SEQ * h + SEQ],
                                         b[:, h, 0:w], start=(k == 0), stop=(k == 2),
                                         skip_group_check=True)
                m.then_inc(A["o"], 1)

            def turn_values(t):
                upto(e, "on", t)
                upto(e, "olo", t - 1)
                if t + 4 - LAG > 0:
                    e.wait_ge(d_mc, t + 4 - LAG)
                for b in range(BPT):
                    m = e.transpose(B4[:, P * b:P * b + P],
                                    on[:, b, :, :].rearrange("p g d -> p (g d)"), ident)
                m.then_inc(A["ot"], 1)

            def out_project(t):
                upto(e, "olo", t)
                e.wait_ge(s_wlo, 4)
                upto(e, "x1", t - 1)
                for j in range(BPT):
                    for k, (a, b) in enumerate(((o_hi, wo_hi), (o_hi, wo_lo), (o_lo, wo_hi))):
                        m = e.matmul(B6, a[:, j, :], b[:, j, :], start=(j == 0 and k == 0),
                                     stop=(j == BPT - 1 and k == 2))
                m.then_inc(A["r"], 1)

            def turn_qk(t, src, done, into, name):
                upto(e, done, t)
                e.wait_ge(s_masks, 16)
                for c in range(KC):
                    m = e.transpose(into[:, P * c:P * c + P], src[:, P * c:P * c + P], ident)
                m.then_inc(A[name], 1)

            def scores(t):
                for n in ("qhi", "qlo", "kxhi", "kxlo"):
                    upto(e, n, t)
                upto(e, "on", t - 2)
                for c in range(KC):
                    dst = pair[:, c // 2, 256 * (c % 2):256 * (c % 2) + 256]
                    for k, (a, b) in enumerate(((q_hi, kx_hi), (q_lo, kx_hi), (q_hi, kx_lo))):
                        for j in range(BPT):
                            m = e.matmul(dst[SEQ * j:SEQ * j + SEQ, :], a[:, c, SEQ * j:SEQ * j + SEQ],
                                         b[:, BPT * c + j, :, :].rearrange("p h k -> p (h k)"),
                                         start=(k == 0), stop=(k == 2), skip_group_check=True)
                m.then_inc(A["s"], 1)

            def turn_slot(s):
                e.wait_ge(d_x[s % 2], 16 * (s // 2 + 1))
                upto(e, "hlo", min(s + LAG + 1, T - 1))
                if s > TAIL:
                    upto(e, "x1", T - 1)
                before = s if s <= TAIL else s - 1
                if before:
                    e.wait_ge(d_tc, before)
                    e.wait_ge(d_tl, min(before, SPLIT))
                for c in range(KC):
                    m = e.transpose(slot_banks(s)[0][:, P * c:P * c + P], xg[s % 2][:, P * c:P * c + P], ident)
                m.then_inc(d_t, 1)

            def adapt_slot(s):
                e.wait_ge(d_tc, s + 1)
                e.wait_ge(d_w2[s % 2], 16 * (s // 2 + 1))
                if s < SPLIT:
                    e.wait_ge(d_tl, s + 1)
                    e.wait_ge(d_whi, s + 1)
                    e.wait_ge(d_wlo, s + 1)
                    upto(e, "olo", s + LAG - 4)
                elif s < TAIL:
                    upto(e, "cq", T - 1)
                else:
                    upto(e, "on", T - 1)
                before = s if s < TAIL else s - 1
                if before:
                    e.wait_ge(d_mc, before)
                for c in range(KC):
                    if s < SPLIT:
                        for k, (a, b) in enumerate(((xgT_hi, w2_hi), (xgT_hi, w2_lo), (xgT_lo, w2_hi))):
                            m = e.matmul(slot_banks(s)[1], a[:, P * c:P * c + P], b[:, c, :], start=(c == 0 and k == 0),
                                         stop=(c == KC - 1 and k == 2))
                    else:
                        m = e.matmul(slot_banks(s)[1], xgT[s % 2][:, P * c:P * c + P], w2t[s % 2][:, c, :],
                                     start=(c == 0), stop=(c == KC - 1))
                m.then_inc(d_m, 1)

            def latent():
                e.wait_ge(m_fc, 64)
                e.wait_ge(d_mc, TAIL)
                upto(e, "qT", T - 1)
                for m_ in range(LC):
                    for k in range(LC):
                        m = e.matmul((B2, B3)[m_], ex_sb[:, k, P * m_:P * m_ + P], fc1_sb[:, k, :],
                                     start=(k == 0), stop=(k == LC - 1))
                    m.then_inc(m_lat, 1)

            def make_route(c):
                e.wait_ge(m_latc, LC)
                if c >= 2:
                    e.wait_ge(m_lo, made(f"route{c - 2}"))
                for k in range(LC):
                    m = e.matmul((B2, B3)[c % 2], latT[:, k, P * c:P * c + P], fc2_sb[:, k, :],
                                 start=(k == 0), stop=(k == LC - 1))
                m.then_inc(m_route, 1)

            def turn(m, c):
                n = KC * m + c
                if n == 0:
                    upto(e, "kT", T - 1)
                    upto(e, "olo", T - 1)
                if c == 0:
                    e.wait_ge(f_y[m % 2], 16 * (m // 2 + 1))
                    if m:
                        e.wait_ge(S["gtc"], m)
                        e.wait_ge(S["gc"], m)
                if n >= 2:
                    e.wait_ge(S["lo"], n - 1)
                for t in range(GROUP):
                    k = e.transpose((B4, B5)[c % 2][:, P * t:P * t + P],
                                    yt[m % 2][:, t, P * c:P * c + P], ident)
                k.then_inc(S["t"], 1)

            def gate_products(m):
                e.wait_ge(S["lo"], KC * (m + 1))
                e.wait_ge(m_lo, made("gate"))
                for c in range(KC):
                    w = gate_hl[:, c, :, :].rearrange("p a n -> p (a n)")
                    for n, y in enumerate((yT_hi, yT_lo)):
                        k = e.matmul(B4[0:2 * EXPERTS, :], w, y[m % 2][:, c, :],
                                     start=(c == 0 and n == 0), stop=(c == KC - 1 and n == 1))
                k.then_inc(S["g"], 1)

            def turn_gates(m):
                e.wait_ge(S["gc"], m + 1)
                for t in range(GROUP):
                    k = e.transpose(B5[:, 2 * EXPERTS * t:2 * EXPERTS * (t + 1)],
                                    gates[:, P * t:P * t + P], cst[0:2 * EXPERTS, C_IDENT:C_IDENT + 2 * EXPERTS])
                k.then_inc(S["gt"], 1)

            def up(m, f):
                n = FC * m + f
                if f == 0:
                    e.wait_ge(S["lo"], KC * (m + 1))
                if n == 0:
                    e.wait_ge(m_lo, made("route3"))
                if n >= 2:
                    e.wait_ge(S["relu"], n - 1)
                cols = slice(P * f, P * f + P)
                for c in range(KC):
                    for k, (a, b) in enumerate(((up_hi, yT_hi), (up_hi, yT_lo), (up_lo, yT_hi))):
                        i = e.matmul((B2, B3)[n % 2], a[:, c, cols], b[m % 2][:, c, :],
                                     start=(c == 0 and k == 0), stop=(c == KC - 1 and k == 2))
                i.then_inc(S["u"], 1)

            def down(m, t):
                n = GROUP * m + t
                toks = slice(P * t, P * t + P)
                if n == 0:
                    e.wait_ge(m_lo, ALL_MADE)
                    e.wait_ge(d_tc, SLOTS)
                    e.wait_ge(d_mc, SLOTS)
                if n >= 2:
                    e.wait_ge(S["tot"], n - 1)
                for c in range(KC):
                    for k, (a, b) in enumerate(((yT_hi, route_hi), (yT_hi, route_lo), (yT_lo, route_hi))):
                        i = e.matmul((B6, B7)[n % 2], a[m % 2][:, c, toks], b[:, c, :],
                                     start=(c == 0 and k == 0), stop=(c == KC - 1 and k == 2))
                i.then_inc(S["rp"], 1)
                for f in range(FC):
                    if t == 0:
                        e.wait_ge(S["ulo"], FC * m + f + 1)
                    for k, (a, b) in enumerate(((u_hi, down_hi), (u_hi, down_lo), (u_lo, down_hi))):
                        i = e.matmul(pair[:, n % 2, :], a[:, f, toks], b[:, f, :],
                                     start=(f == 0 and k == 0), stop=(f == FC - 1 and k == 2))
                i.then_inc(S["dr"], 1)

            e.wait_ge(s_t, STEP_AT_RANK)
            for j in range(BPT):
                q = slice(SEQ * j, SEQ * j + SEQ)
                e.matmul(B2[q, 0:TILES], cst[:, C_VAL:C_COL], at_rank[:, j::BPT], start=True, stop=True)
                m = e.matmul(B3[q, 0:TILES], style_of[:, :], at_rank[:, j::BPT], start=True, stop=True)
            m.then_inc(s_tp, 1)
            e.wait_ge(s_t, STEP_FIRST)
            e.matmul(B4[:, 0:1], after[:, :], first[:, :], start=True, stop=True).then_inc(s_tp, 1)
            e.wait_ge(s_t, STEP_ONEHOT)
            for j in range(BPT):
                e.matmul(B5[SEQ * j:SEQ * j + SEQ, 0:SLOTS], row_of[:, :], onehot[:, j::BPT],
                         start=True, stop=True)
            e.matmul(B6[0:1, 0:SLOTS], idc[:, :], onehot[:, 0::BPT], start=True, stop=True) \
                .then_inc(s_tp, 1)
            e.wait_ge(s_tables, 2)

            style(0)
            for i in range(STEPS):
                live = lambda t: 0 <= t < T
                slot = i >= LAG
                drain = i >= T
                if 0 < i < T - 1:
                    style(i + 1)
                if live(i):
                    upto(e, "cq", i - 1)
                    project(i, 0, B2, "pq")
                if i == 0:
                    style(1)
                if drain:
                    turn_slot(i - LAG)
                if live(i - 4):
                    values(i - 4)
                if live(i):
                    upto(e, "ck", i - 1)
                    upto(e, "qT", i - 2)
                    project(i, 1, B3, "pk")
                if live(i - 4):
                    turn_values(i - 4)
                if drain:
                    adapt_slot(i - LAG)
                if live(i):
                    upto(e, "cv", i - 1)
                    upto(e, "kT", i - 2)
                    project(i, 2, B5, "pv")
                if slot and not drain:
                    turn_slot(i - LAG)
                if live(i - 4):
                    out_project(i - 4)
                if live(i - 1):
                    upto(e, "ck", min(i, T - 1))
                    turn_qk(i - 1, qn[(i - 1) % 2], "qn", B3, "tq")
                    upto(e, "cv", min(i, T - 1))
                    turn_qk(i - 1, kn[(i - 1) % 2], "kn", B5, "tk")
                if slot and not drain:
                    adapt_slot(i - LAG)
                if live(i - 2):
                    scores(i - 2)

            for s in range(TAIL, SLOTS):
                k = s - TAIL
                if k < 2:
                    turn_slot(s)
                if k and s + 1 < SLOTS:
                    turn_slot(s + 1)
                if k == 0:
                    latent()
                adapt_slot(s)
                if k < 2:
                    make_route(2 * k)
                    make_route(2 * k + 1)
                if k == 0:
                    for c in range(KC):
                        turn(0, c)
                if k == 2:
                    gate_products(0)
                if k == 3:
                    turn_gates(0)

            for m in range(GROUPS):
                ahead = m + 1 < GROUPS
                for f in range(FC):
                    up(m, f)
                    if ahead and 0 <= f - 2 < KC:
                        turn(m + 1, f - 2)
                if ahead:
                    gate_products(m + 1)
                for t in range(GROUP):
                    down(m, t)
                    if ahead and t == 0:
                        turn_gates(m + 1)

        @block.scalar
        def _(e):
            def high(name):
                (ready, value), src, hi, _ = parts[name]
                e.wait_ge(ready, value)
                e.activation(hi, src, ACT.Copy).then_inc(m_hi, 1)

            def slot_in(s):
                e.wait_ge(d_t, s + 1)
                upto_product(e, s)
                dst = xgT_hi if s < SPLIT else xgT[s % 2]
                e.activation(dst[:, :], slot_banks(s)[0], ACT.Copy).then_inc(d_tc, 1)

            def high_w2(s):
                e.wait_ge(d_w2[s % 2], 16 * (s // 2 + 1))
                e.activation(w2_hi[:, :, :], w2t[0][:, :, :], ACT.Copy).then_inc(d_whi, 1)

            def slot_out(s):
                e.wait_ge(d_m, s + 1)
                if s >= 2:
                    e.wait_ge(d_y[s % 2], 16 * (s // 2))
                e.activation(ys[s % 2][:, :], slot_banks(s)[1], ACT.Copy).then_inc(d_mc, 1)

            def high_y(m, c):
                e.wait_ge(S["t"], KC * m + c + 1)
                if m >= 2 and c == 0:
                    e.wait_ge(S["dr"], GROUP * (m - 1))
                if m == 1 and c == 0:
                    e.wait_ge(m_lo, ALL_MADE)
                e.activation(yT_hi[m % 2][:, c, :], (B4, B5)[c % 2], ACT.Copy).then_inc(S["hi"], 1)

            def gates_out(m):
                e.wait_ge(S["g"], m + 1)
                if m:
                    e.wait_ge(S["gt"], m)
                e.activation(gates[:, :], B4[0:2 * EXPERTS, :], ACT.Copy).then_inc(S["gc"], 1)

            def softmax(t):
                upto(e, "sub", t)
                e.activation(probs[:, :, :], probs[:, :, :], ACT.Exp).then_inc(A["exp"], 1)
                if 0 <= t + 3 - LAG < SPLIT:
                    high_w2(t + 3 - LAG)
                upto(e, "pT", t)
                upto(e, "o", t - 1)
                e.activation(p_hi[:, :], probsT[:, :], ACT.Copy).then_inc(A["phi"], 1)

            def high_o(t):
                upto(e, "ot", t)
                upto(e, "r", t - 1)
                e.activation(o_hi[:, :, :].rearrange("p j (b q) -> p j b q", b=BPT),
                             B4.rearrange("p (b j q) -> p j b q", b=BPT, j=BPT), ACT.Copy) \
                    .then_inc(A["ohi"], 1)

            def high_h(t):
                upto(e, "h", t)
                upto(e, "pv", t - 2)
                e.activation(h_hi[t % 2][:, :, :], B7.rearrange("p (c t) -> p c t", c=KC), ACT.Copy) \
                    .then_inc(A["hhi"], 1)

            def high_weights(n):
                e.wait_ge(s_stage[n], 16)
                dst = wqkv_hi[:, n] if n < 3 else wo_hi[:, :, :]
                e.activation(dst, stage[n][:, :, :], ACT.Copy).then_inc(s_whi, 1)

            high_weights(0)
            high_weights(1)
            high_h(0)
            high_weights(2)
            for i in range(STEPS):
                live = lambda t: 0 <= t < T
                t = i - 2
                if live(t):
                    upto(e, "tq", t)
                    upto(e, "qlo", t - 1)
                    for c in range(KC):
                        m = e.activation(qT[:, c, :], B3[:, P * c:P * c + P], ACT.Identity,
                                         bias=qkln[:, KC + c:KC + c + 1], scale=qkln[:, c:c + 1])
                    m.then_inc(A["qT"], 1)
                if live(i + 1):
                    high_h(i + 1)
                if i == 0:
                    high_weights(3)
                t = i - 2
                if live(t):
                    upto(e, "tk", t)
                    upto(e, "klo", t - 1)
                    for c in range(KC):
                        m = e.activation(kT[:, c, :], B5[:, P * c:P * c + P], ACT.Identity,
                                         bias=qkln[:, 3 * KC + c:3 * KC + c + 1],
                                         scale=qkln[:, 2 * KC + c:2 * KC + c + 1])
                    m.then_inc(A["kT"], 1)
                    upto(e, "kT", t)
                    upto(e, "kxlo", t - 1)
                    e.activation(k_hi[:, :], kT[:, :, :].rearrange("p c t -> p (c t)"), ACT.Copy) \
                        .then_inc(A["khi"], 1)
                    upto(e, "qT", t)
                    upto(e, "s", t - 1)
                    e.activation(q_hi[:, :, :], qT[:, :, :], ACT.Copy).then_inc(A["qhi"], 1)
                if i >= T:
                    slot_in(i - LAG)
                    high_o(i - 4)
                if live(i - 3):
                    softmax(i - 3)
                if live(i - 4) and i < T:
                    high_o(i - 4)
                if LAG <= i < T:
                    slot_in(i - LAG)
                if live(i):
                    t = i
                    upto(e, "shift", t)
                    for n, buf in enumerate((qn, kn)):
                        b = buf[t % 2]
                        e.activation(b[:, :], b[:, :], ACT.Identity, bias=shift[t % 2][:, n:n + 1],
                                     scale=rstd[t % 2][:, n:n + 1]).then_inc(A[("qn", "kn")[n]], 1)
                    upto(e, "cv", t)
                    upto(e, "vxhi", t - VR)
                    e.activation(v_hi[t % VR][:, :, :], vf[t % 2][:, :].rearrange("p (h d) -> p h d", h=HEADS),
                                 ACT.Copy).then_inc(A["vhi"], 1)
                if i >= LAG:
                    slot_out(i - LAG)

            for s in range(TAIL, SLOTS):
                k = s - TAIL
                if k < 2:
                    slot_in(s)
                if k and s + 1 < SLOTS:
                    slot_in(s + 1)
                if k == 0:
                    upto(e, "x1", T - 1)
                    high("gate")
                    e.wait_ge(m_lat, LC)
                    for m_ in range(LC):
                        m = e.activation(latT[:, m_, :], (B2, B3)[m_], ACT.Copy)
                    m.then_inc(m_latc, LC)
                slot_out(s)
                if k == 0:
                    high("route0")
                    high("route1")
                    for c in range(KC):
                        high_y(0, c)
                if k == 1:
                    for name in ("up0", "up1", "route2", "route3"):
                        high(name)
                if k == 2:
                    gates_out(0)
                if k == 3:
                    high("down0")
                if s == SLOTS - 1:
                    high("down1")

            for n in range(2):
                e.wait_ge(a_store[n], 16 * (T // 2))
            for m in range(GROUPS):
                ahead = m + 1 < GROUPS
                for f in range(FC + 1):
                    n = FC * m + f
                    if f < FC:
                        e.wait_ge(S["u"], n + 1)
                        if n >= 3:
                            e.wait_ge(S["ulo"], n - 2)
                        e.activation(act[n % 3][:, :], (B2, B3)[n % 2], ACT.Relu).then_inc(S["relu"], 1)
                    if f:
                        e.wait_ge(S["act"], n)
                        if n == 1:
                            e.wait_ge(m_lo, ALL_MADE)
                        if m and f == 1:
                            e.wait_ge(S["dr"], GROUP * m)
                        e.activation(u_hi[:, f - 1, :], act[(n - 1) % 3][:, :], ACT.Copy).then_inc(S["uhi"], 1)
                    if ahead and 0 <= f - 2 < KC:
                        high_y(m + 1, f - 2)
                if ahead:
                    gates_out(m + 1)
                for t in range(GROUP):
                    n = GROUP * m + t
                    e.wait_ge(S["rp"], n + 1)
                    e.wait_ge(S["w"], m + 1)
                    if n < 2:
                        e.wait_ge(d_y[n], 16 * (SLOTS // 2))
                    if n >= 2:
                        e.wait_ge(S["res"], n - 1)
                    e.activation(total[n % 2][:, :], (B6, B7)[n % 2], ACT.Identity,
                                 scale=weight[m % 2][:, t:t + 1]).then_inc(S["route"], 1)

        @block.vector
        def _(e):
            def clip(t, src, dst, name):
                e.tensor_scalar(dst, src, CLIP, -CLIP, ALU.min, ALU.max).then_inc(A[name], 1)

            def low(name):
                _, src, hi, lo = parts[name]
                e.wait_ge(m_hi, made(name))
                e.tensor_tensor(lo, src, hi.bitcast(F32), ALU.subtract).then_inc(m_lo, 1)

            def low_y(m, c):
                e.wait_ge(S["hi"], KC * m + c + 1)
                e.tensor_tensor(yT_lo[m % 2][:, c, :], (B4, B5)[c % 2], yT_hi[m % 2][:, c, :].bitcast(F32),
                                ALU.subtract).then_inc(S["lo"], 1)

            def gate_weights(m):
                e.wait_ge(S["gt"], m + 1)
                e.tensor_copy(gates_t[:, :, :], B5[:, 0:GROUP * 2 * EXPERTS]
                              .rearrange("p (t n) -> p t n", t=GROUP)).then_inc(S["gtc"], 1)
                e.wait_ge(S["gtc"], m + 1)
                e.tensor_tensor(logits[:, :, :], gates_t[:, :, 0:EXPERTS], gates_t[:, :, EXPERTS:2 * EXPERTS],
                                ALU.add).then_inc(S["log"], 1)
                e.wait_ge(S["log"], m + 1)
                for t in range(GROUP):
                    k = e.max(best[:, t, :], logits[:, t, :])
                k.then_inc(S["best"], 1)
                e.wait_ge(S["best"], m + 1)
                e.tensor_tensor(weight[m % 2][:, :], best[:, :, 0], best[:, :, 1], ALU.add).then_inc(S["w"], 1)

            def low_h(t):
                upto(e, "hhi", t)
                upto(e, "pv", t - 2)
                e.tensor_tensor(h_lo[t % 2][:, :, :], B7.rearrange("p (c t) -> p c t", c=KC),
                                h_hi[t % 2][:, :, :].bitcast(F32), ALU.subtract).then_inc(A["hlo"], 1)

            def turn_probs(t):
                upto(e, "exp", t)
                upto(e, "plo", t - 1)
                e.transpose(probsT[:, :], probs[:, :, :].rearrange("p h k -> p (h k)")).then_inc(A["pT"], 1)

            def low_o(t):
                upto(e, "ohi", t)
                upto(e, "r", t - 1)
                e.tensor_tensor(o_lo[:, :, :].rearrange("p j (b q) -> p j b q", b=BPT),
                                B4.rearrange("p (b j q) -> p j b q", b=BPT, j=BPT),
                                o_hi[:, :, :].bitcast(F32).rearrange("p j (b q) -> p j b q", b=BPT),
                                ALU.subtract).then_inc(A["olo"], 1)

            steps = [0]

            def step(i):
                i.then_inc(s_t, 1)
                steps[0] += 1
                e.wait_ge(s_t, steps[0])

            e.wait_ge(s_cst, 16)
            e.wait_ge(s_ids, 64)
            row, col, pmod = cst[:, C_ROW:C_SLOT], cst[:, C_COL:C_COL + 1], cst[:, C_PMOD:C_PMOD + 1]
            step(e.tensor_copy(idr[:, :], ids_row[:, :]))
            step(e.tensor_copy(idc[:, :], ids_col[:, :]))
            step(e.tensor_copy(stylec[:, :], style_col[:, :]))
            step(e.scalar_tensor_tensor(keyr[:, :], idr[:, :], float(BATCHES), row, ALU.mult, ALU.add))
            step(e.scalar_tensor_tensor(keyc[:, :], idc[:, :], float(BATCHES), col, ALU.mult, ALU.add))
            step(e.tensor_scalar(before[:, :], keyr[:, :], keyc[:, 0:1], None, ALU.is_lt))
            step(e.tensor_reduce(rank[:, :], before[:, :], AX.X, ALU.add))
            step(e.tensor_scalar(at_rank[:, :], row, rank[:, 0:1], None, ALU.is_equal))
            spread = cst[:, C_VAL:C_COL]
            step(e.tensor_scalar(style_of[:, :], spread, 0.0, stylec[:, 0:1], ALU.mult, ALU.add))
            assert steps[0] == STEP_AT_RANK
            step(e.tensor_scalar(sorted_row[:, :], rank[:, :], float(SEQ), -ABSENT, ALU.mult, ALU.add))
            step(e.tensor_scalar(row_of[:, :], spread, 0.0, sorted_row[:, 0:1], ALU.mult, ALU.add))
            e.wait_ge(s_tp, 1)
            step(e.tensor_scalar(table_f[0][:, 0:TILES], B2[:, 0:TILES], ABSENT, pmod, ALU.add, ALU.add))
            step(e.tensor_scalar(table_f[1][:, 0:TILES], B3[:, 0:TILES], float(SEQ), pmod, ALU.mult, ALU.add))
            e.tensor_copy(tile_rows[:, :], table_f[0][:, 0:TILES])
            e.tensor_copy(style_idx[:, :], table_f[1][:, 0:TILES]).then_inc(s_tables, 1)
            step(e.tensor_scalar(after[:, :], keyr[:, :], keyc[:, 0:1], None, ALU.is_gt))
            step(e.tensor_scalar(same[:, :], idr[:, :], idc[:, 0:1], None, ALU.is_equal))
            step(e.tensor_tensor(same[:, :], same[:, :], before[:, :], ALU.mult))
            step(e.tensor_reduce(within[:, :], same[:, :], AX.X, ALU.add))
            step(e.tensor_copy(within_i[:, :], within[:, :]))
            step(e.tensor_scalar(place_i[:, :], within_i[:, :], BPT - 1, None, ALU.bitwise_and))
            step(e.tensor_copy(place[:, :], place_i[:, :]))
            step(e.tensor_scalar(first[:, :], place[:, :], 0.0, None, ALU.is_equal))
            assert steps[0] == STEP_FIRST
            e.wait_ge(s_tp, 2)
            step(e.scalar_tensor_tensor(slot_no[:, :], B4[:, 0:1], -1.0, first[:, :], ALU.add, ALU.add))
            step(e.scalar_tensor_tensor(column[:, :], slot_no[:, :], float(BPT), place[:, :],
                                        ALU.mult, ALU.add))
            step(e.tensor_scalar(onehot[:, :], cst[:, C_SLOT:C_VAL], column[:, 0:1], None, ALU.is_equal))
            assert steps[0] == STEP_ONEHOT
            e.wait_ge(s_tp, 3)
            step(e.tensor_scalar(table_f[2][:, :], B5[:, 0:SLOTS], ABSENT, pmod, ALU.add, ALU.add))
            step(e.tensor_copy(table_f[3][0:1, :], B6[0:1, 0:SLOTS]))
            step(e.tensor_copy(slot_rows[:, :], table_f[2][:, :]))
            e.tensor_copy(slot_adapter[:, :], table_f[3][0:1, :]).then_inc(s_tables, 1)
            def low_weights(n):
                e.wait_ge(s_whi, n + 1)
                hi, dst = (wqkv_hi[:, n], wqkv_lo[:, n]) if n < 3 else (wo_hi[:, :, :], wo_lo[:, :, :])
                e.tensor_tensor(dst, stage[n][:, :, :], hi.bitcast(F32), ALU.subtract).then_inc(s_wlo, 1)

            def finish_start():
                low_weights(3)
                e.wait_ge(s_masks, 16)
                e.tensor_copy(kmask[:, :], cst[:, C_KMASK:C_VMASK]).then_inc(A["mask"], 1)
                e.tensor_copy(vmask[:, :], cst[:, C_VMASK:C_WMASK]).then_inc(A["mask"], 1)
                e.wait_ge(s_wlo, 4)
                e.wait_ge(s_tables, 2)
                e.wait_ge(A["mask"], 2)
                e.tensor_copy(vx_hi[:, :, BPT * HD:VW], vmask[:, BPT * HD:VW].rearrange("p (o b) -> p o b", o=1)
                              .broadcast_to([P, HEADS, BPT])).then_inc(A["vx1"], 1)

            low_weights(0)
            low_h(0)
            low_weights(1)
            low_weights(2)
            e.wait_ge(s_wlo, 3)
            for i in range(STEPS):
                live = lambda t: 0 <= t < T
                t = i - 3
                if live(t):
                    upto(e, "s", t)
                    upto(e, "pT", t - 1)
                    for n in range(2):
                        h = slice(16 * n, 16 * n + 16)
                        e.scalar_tensor_tensor(probs[:, h, :], pair[:, n, :].rearrange("p (h k) -> p h k", k=SEQ),
                                               SCALE, bias[:, h, :], ALU.mult, ALU.add).then_inc(A["sb"], 1)
                if live(i + 1):
                    low_h(i + 1)
                t = i - 3
                if live(t):
                    upto(e, "sb", t)
                    upto(e, "sub", t - 1)
                    e.tensor_reduce(row_max[:, :], probs[:, :, :], AX.X, ALU.max).then_inc(A["max"], 1)
                if live(i):
                    t = i
                    upto(e, "pq", t)
                    upto(e, "tq", t - 2)
                    clip(t, B2, qn[t % 2][:, :], "cq")
                    upto(e, "cq", t)
                    e.bn_stats(stats[t % 2][:, 0, :], qn[t % 2][:, :]).then_inc(A["bn"], 1)
                t = i - 4
                if live(t):
                    upto(e, "o", t)
                    o4 = pair[:, :, 0:4 * VW].rearrange("p n (g v) -> p n g v", g=4)
                    e.reciprocal(recip[:, :, :, :], o4[:, :, :, BPT * HD:VW]).then_inc(A["rec"], 1)
                    upto(e, "rec", t)
                    upto(e, "ot", t - 1)
                    for n in range(2):
                        e.tensor_tensor(on[:, :, 4 * n:4 * n + 4, :].rearrange("p b g d -> p g b d"),
                                        o4[:, n, :, 0:BPT * HD].rearrange("p g (b d) -> p g b d", b=BPT),
                                        recip[:, n, :, :].rearrange("p g (b o) -> p g b o", o=1)
                                        .broadcast_to([P, 4, BPT, HD]), ALU.mult).then_inc(A["on"], 1)
                if i >= T:
                    low_o(i - 4)
                if live(i - 3) and i > 3:
                    turn_probs(i - 3)
                t = i - 2
                if live(t):
                    upto(e, "khi", t)
                    upto(e, "s", t - 1)
                    wide = lambda a: a[:, :].rearrange("p (n o k) -> p n o k", o=1, k=SEQ) \
                        .broadcast_to([P, KC * BPT, HPC, SEQ])
                    mask = kmask[:, :].rearrange("p (o h k) -> p o h k", o=1, h=HPC) \
                        .broadcast_to([P, KC * BPT, HPC, SEQ])
                    e.tensor_tensor(kx_hi[:, :, :, :], wide(k_hi), mask, ALU.mult).then_inc(A["kxhi"], 1)
                if live(i - 4) and i < T:
                    low_o(i - 4)
                t = i - 2
                if live(t):
                    e.tensor_tensor(k_lo[:, :], kT[:, :, :].rearrange("p c t -> p (c t)"), k_hi[:, :],
                                    ALU.subtract).then_inc(A["klo"], 1)
                if live(i):
                    t = i
                    upto(e, "pk", t)
                    upto(e, "tk", t - 2)
                    clip(t, B3, kn[t % 2][:, :], "ck")
                    upto(e, "ck", t)
                    e.bn_stats(stats[t % 2][:, 1, :], kn[t % 2][:, :]).then_inc(A["bn"], 1)
                    upto(e, "bn", t)
                    for n in range(2):
                        m = e.bn_aggr(mean_var[t % 2][:, n, :], stats[t % 2][:, n, :])
                    m.then_inc(A["aggr"], 1)
                    upto(e, "aggr", t)
                    e.tensor_scalar(var_eps[t % 2][:, :], mean_var[t % 2][:, :, 1], EPS, None, ALU.add) \
                        .then_inc(A["eps"], 1)
                    upto(e, "pv", t)
                    upto(e, "vlo", t - 2)
                    clip(t, B5, vf[t % 2][:, :], "cv")
                if 0 <= i - LAG < SPLIT:
                    e.wait_ge(d_tc, i - LAG + 1)
                    e.tensor_tensor(xgT_lo[:, :], B7, xgT_hi[:, :].bitcast(F32), ALU.subtract) \
                        .then_inc(d_tl, 1)
                t = i - 2
                if live(t):
                    upto(e, "klo", t)
                    e.tensor_tensor(kx_lo[:, :, :, :], wide(k_lo), mask, ALU.mult).then_inc(A["kxlo"], 1)
                    upto(e, "qhi", t)
                    e.tensor_tensor(q_lo[:, :, :], qT[:, :, :], q_hi[:, :, :], ALU.subtract) \
                        .then_inc(A["qlo"], 1)
                if i == 3:
                    turn_probs(0)
                if live(i):
                    t = i
                    upto(e, "rstd", t)
                    upto(e, "kn", t - 2)
                    e.scalar_tensor_tensor(shift[t % 2][:, :], mean_var[t % 2][:, :, 0], -1.0,
                                           rstd[t % 2][:, :], ALU.mult, ALU.mult).then_inc(A["shift"], 1)
                t = i - 3
                if live(t):
                    upto(e, "vlo", t)
                    upto(e, "vhi", t)
                    upto(e, "o", t - 1)
                    dims = [P, HEADS, BPT, HD]
                    own = vmask[:, 0:BPT * HD].rearrange("p (o b d) -> p o b d", o=1, b=BPT).broadcast_to(dims)
                    for vx, v, name in ((vx_hi, v_hi[t % VR], "vxhi"), (vx_lo, v_lo[t % VR], "vxlo")):
                        e.tensor_tensor(vx[:, :, 0:BPT * HD].rearrange("p h (b d) -> p h b d", b=BPT),
                                        v[:, :, :].rearrange("p h (o d) -> p h o d", o=1).broadcast_to(dims),
                                        own, ALU.mult).then_inc(A[name], 1)
                t = i - 4
                if live(t):
                    upto(e, "r", t)
                    if t >= 2:
                        e.wait_ge(a_store[t % 2], 16 * (t // 2))
                    e.tensor_tensor(x1t[t % 2][:, :], B6, xt[t % XR][:, :], ALU.add).then_inc(A["x1"], 1)
                if i == 0:
                    finish_start()

            for name in ("gate", "route0", "route1"):
                low(name)
            for c in range(KC):
                low_y(0, c)
            for name in ("up0", "up1", "route2", "route3"):
                low(name)
            gate_weights(0)
            low("down0")
            low("down1")

            for m in range(GROUPS):
                for f in range(FC):
                    n = FC * m + f
                    e.wait_ge(S["relu"], n + 1)
                    e.tensor_tensor(act[n % 3][:, :], act[n % 3][:, :], act[n % 3][:, :], ALU.mult) \
                        .then_inc(S["act"], 1)
                    if m + 1 < GROUPS and 0 <= f - 2 < KC:
                        low_y(m + 1, f - 2)
                for t in range(GROUP):
                    n = GROUP * m + t
                    b = n % 2
                    if n == 0:
                        e.wait_ge(f_ln, 16)
                    e.wait_ge(f_x1[t], 16 * (m + 1))
                    e.tensor_tensor(x1g[t], x1g[t], lnw[:, 1, :], ALU.add).then_inc(S["bet"], 1)
                    e.wait_ge(S["route"], n + 1)
                    e.wait_ge(S["dr"], n + 1)
                    e.tensor_tensor(total[b][:, :], total[b][:, :], pair[:, b, :], ALU.add) \
                        .then_inc(S["tot"], 1)
                    e.wait_ge(S["tot"], n + 1)
                    e.bn_stats(fstats[:, :], total[b][:, :]).then_inc(S["bn"], 1)
                    e.wait_ge(S["bn"], n + 1)
                    e.bn_aggr(fmv[b][:, :], fstats[:, :]).then_inc(S["aggr"], 1)
                    e.wait_ge(S["aggr"], n + 1)
                    e.tensor_scalar(fve[b][:, :], fmv[b][:, 1:2], EPS, None, ALU.add).then_inc(S["eps"], 1)
                    e.scalar_tensor_tensor(total[b][:, :], total[b][:, :], fmv[b][:, 0:1], lnw[:, 0, :],
                                           ALU.subtract, ALU.mult).then_inc(S["gam"], 1)
                    e.wait_ge(S["gam"], n + 1)
                    e.wait_ge(S["bet"], n + 1)
                    e.wait_ge(S["rstd"], n + 1)
                    if n >= 3:
                        e.wait_ge(f_out[n % 3], 16 * (n // 3))
                    e.scalar_tensor_tensor(ot[n % 3][:, :], total[b][:, :], frstd[b][:, 0:1], x1g[t],
                                           ALU.mult, ALU.add).then_inc(S["res"], 1)
                    if t == 0 and m + 1 < GROUPS:
                        gate_weights(m + 1)

        @block.gpsimd
        def _(e):
            def style(t):
                upto(e, "h", t - 2)
                e.wait_ge(a_x[t % XR], 32 * (t // XR + 1))
                e.tensor_tensor(style_bd[t % 2][:, :, :],
                                style_rows[t % XR][:, :].rearrange("p (o d) -> p o d", o=1)
                                .broadcast_to([P, BPT, SEQ]),
                                cst[:, C_WMASK:C_ROW].rearrange("p (j d) -> p j d", j=BPT), ALU.mult) \
                    .then_inc(A["style"], 1)

            def rows(idx, i):
                return bass.IndirectOffsetOnAxis(ap=idx[:, i:i + 1], axis=0)

            def gather(t):
                upto(e, "x1", t - XR)
                e.indirect_dma_start(out=xt[t % XR][:, :], out_offset=None, in_=x, in_offset=rows(tile_rows, t)) \
                    .then_inc(a_x[t % XR], 16)
                e.indirect_dma_start(out=style_rows[t % XR][:, :], out_offset=None, in_=style_w,
                                     in_offset=rows(style_idx, t)).then_inc(a_x[t % XR], 16)

            def gather_slot(s):
                last = min(s, T - 1)
                for n in (last, last - 1):
                    if n >= 0:
                        e.wait_ge(a_store[n % 2], 16 * (n // 2 + 1))
                if s >= 2:
                    e.wait_ge(d_t, s - 1)
                there = P * (last + 1)
                e.indirect_dma_start(out=xg[s % 2][:, :], out_offset=None, in_=x1_rows[0:there, :],
                                     in_offset=rows(slot_rows, s), bounds_check=there - 1,
                                     oob_is_err=False).then_inc(d_x[s % 2], 16)

            def scatter_slot(s):
                e.wait_ge(d_mc, s + 1)
                e.indirect_dma_start(out=y_rows, out_offset=rows(slot_rows, s), in_=ys[s % 2][:, :],
                                     in_offset=None, bounds_check=TOKENS - 1,
                                     oob_is_err=False).then_inc(d_y[s % 2], 16)

            def store(n):
                e.wait_ge(S["res"], n + 1)
                e.indirect_dma_start(out=out, out_offset=bass.IndirectOffsetOnAxis(
                    ap=tile_rows[:, n:n + 1], axis=0), in_=ot[n % 3][:, :], in_offset=None) \
                    .then_inc(f_out[n % 3], 16)

            for n in range(2):
                e.memset(xg[n][:, :], 0.0).then_inc(d_zero, 1)
            e.wait_ge(d_zero, 2)
            e.wait_ge(s_tables, 1)
            for t in range(2):
                gather(t)
            e.wait_ge(s_cst, 16)
            style(0)
            gather(2)
            style(1)
            for i in range(STEPS):
                live = lambda t: 0 <= t < T
                t = i - 3
                if live(t):
                    upto(e, "max", t)
                    e.tensor_tensor(probs[:, :, :], probs[:, :, :],
                                    row_max[:, :].rearrange("p (h o) -> p h o", o=1)
                                    .broadcast_to([P, HEADS, SEQ]), ALU.subtract).then_inc(A["sub"], 1)
                if i > LAG:
                    scatter_slot(i - LAG - 1)
                if i >= LAG - 1:
                    gather_slot(i - LAG + 1)
                if live(i + 2):
                    style(i + 2)
                if live(i + 3):
                    gather(i + 3)
                s = i - LAG
                if 0 <= s < SPLIT:
                    e.wait_ge(d_whi, s + 1)
                    e.tensor_tensor(w2_lo[:, :, :], w2t[0][:, :, :], w2_hi[:, :, :].bitcast(F32),
                                    ALU.subtract).then_inc(d_wlo, 1)
                if live(i):
                    upto(e, "eps", i)
                    e.tensor_tensor(rstd[i % 2][:, :], var_eps[i % 2][:, :], cst[:, C_POW:C_POW + 2], ALU.pow) \
                        .then_inc(A["rstd"], 1)
                if live(t):
                    upto(e, "phi", t)
                    upto(e, "o", t - 1)
                    e.tensor_tensor(p_lo[:, :], probsT[:, :], p_hi[:, :], ALU.subtract).then_inc(A["plo"], 1)
                if live(i):
                    t = i
                    upto(e, "vhi", t)
                    upto(e, "vxlo", t - VR)
                    e.tensor_tensor(v_lo[t % VR][:, :, :], vf[t % 2][:, :].rearrange("p (h d) -> p h d", h=HEADS),
                                    v_hi[t % VR][:, :, :], ALU.subtract).then_inc(A["vlo"], 1)
            gather_slot(TAIL + 1)
            scatter_slot(TAIL - 1)
            gather_slot(TAIL + 2)
            for s in range(TAIL, SLOTS):
                if s + 3 < SLOTS:
                    gather_slot(s + 3)
                scatter_slot(s)

            for m in range(GROUPS):
                for f in range(FC):
                    n = FC * m + f
                    e.wait_ge(S["uhi"], n + 1)
                    if n == 0:
                        e.wait_ge(m_lo, ALL_MADE)
                    if m and f == 0:
                        e.wait_ge(S["dr"], GROUP * m)
                    e.tensor_tensor(u_lo[:, f, :], act[n % 3][:, :], u_hi[:, f, :].bitcast(F32), ALU.subtract) \
                        .then_inc(S["ulo"], 1)
                for t in range(GROUP):
                    n = GROUP * m + t
                    e.wait_ge(S["eps"], n + 1)
                    e.tensor_tensor(frstd[n % 2][:, :], fve[n % 2][:, :], cst[:, C_POW:C_POW + 1], ALU.pow) \
                        .then_inc(S["rstd"], 1)
                    if n:
                        store(n - 1)
            store(TILES - 1)
            for n in range(3):
                e.wait_ge(f_out[n], 16 * ((TILES - n + 2) // 3))
    top.close()


def chunked(w):
    return np.ascontiguousarray(w.reshape(-1, P, w.shape[1]).transpose(1, 0, 2))


def kernel(x, itok_B_0_15, itok_B_3_7, L0_cond_weights, L0_attn_w_qkv, L0_attn_q_ln_w, L0_attn_q_ln_b,
           L0_attn_k_ln_w, L0_attn_k_ln_b, L0_attn_w_out, L0_cond2_weight, L0_ffn_gate_w, L0_ffn_up_w,
           L0_ffn_down_w, L0_ffn_fc1_w, L0_ffn_fc2_w, L0_ffn_expert_w, L0_ffn_ln_gamma, L0_ffn_ln_beta):
    import concourse.bacc as bacc
    from concourse.bass_utils import run_bass_kernel_spmd

    a = lambda v: np.asarray(v)
    side = lambda v: a(v).reshape(KC, P).T
    arrays = {
        "x": a(x).reshape(TOKENS, DM),
        "style_ids": a(itok_B_0_15).reshape(1, BATCHES),
        "adapter_ids": a(itok_B_3_7).reshape(1, BATCHES),
        "style_w": a(L0_cond_weights).reshape(STYLES * SEQ, SEQ),
        "wqkv": a(L0_attn_w_qkv).reshape(3, DM, KC, P).transpose(3, 0, 2, 1),
        "wo": a(L0_attn_w_out).reshape(DM, HG, BPT, HD).transpose(1, 3, 2, 0).reshape(P, BPT, DM),
        "qk_ln": np.concatenate([side(v) for v in (L0_attn_q_ln_w, L0_attn_q_ln_b, L0_attn_k_ln_w,
                                                   L0_attn_k_ln_b)], axis=1),
        "w2": a(L0_cond2_weight).reshape(ADAPTERS, DM, KC, P).transpose(3, 0, 2, 1)
        .reshape(P, ADAPTERS, KC * DM),
        "w_up": chunked(a(L0_ffn_up_w)),
        "w_down": chunked(a(L0_ffn_down_w)),
        "fc1t": chunked(a(L0_ffn_fc1_w).T),
        "expert": chunked(a(L0_ffn_expert_w)),
        "fc2": chunked(a(L0_ffn_fc2_w)),
        "gate": chunked(a(L0_ffn_gate_w)),
        "ffn_ln": np.concatenate([a(L0_ffn_ln_gamma), a(L0_ffn_ln_beta)]).reshape(1, 2 * DM),
        "consts": constants(),
    }
    arrays = {n: np.ascontiguousarray(v) for n, v in arrays.items()}
    nc = bacc.Bacc("TRN2", target_bir_lowering=False, num_devices=1)
    aps = {n: nc.dram_tensor(f"in_{n}", v.shape, mybir.dt.from_np(v.dtype), kind="ExternalInput").ap()
           for n, v in arrays.items()}
    aps["out"] = nc.dram_tensor("out", (TOKENS, DM), F32, kind="ExternalOutput").ap()
    program(nc, **aps)
    r = run_bass_kernel_spmd(nc, [{f"in_{n}": v for n, v in arrays.items()}], core_ids=[0])
    return r.results[0]["out"].reshape(BATCHES, SEQ, DM)
```
